# Optimizing a Trainium2 kernel written in Bass

```python
import numpy as np
import jax
import jax.numpy as jnp

def _softmax(x, axis=-1):
    return jax.nn.softmax(x, axis=axis)

def _gelu(x):
    return jax.nn.gelu(x, approximate=True)

def _silu(x):
    return jax.nn.silu(x)

def _sigmoid(x):
    return jax.nn.sigmoid(x)

def _layernorm(x, axis=-1, eps=1e-05):
    m = jnp.mean(x, axis=axis, keepdims=True)
    v = jnp.var(x, axis=axis, keepdims=True)
    return (x - m) / jnp.sqrt(v + eps)

def _scatter_add(tgt, idx, src, axis=0):
    return tgt.at[idx].add(src)

def _segment_sum(src, seg, n):
    return jax.ops.segment_sum(src, seg, n)
kernel_name = 'mk_seq_preln_d1_jaxref_r8_ad2240'

def setup_inputs(seed: int=0):
    np.random.seed(seed)
    _w = jnp.asarray

    def _L0_attn_setup():
        import jax, jax.numpy as jnp
        import numpy as np
        B, S, D, H, R = (2, 256, 128, 16, 64)
        HD = D // H
        VOCAB = 2 * R + 1
        key = jax.random.key(seed)
        ks = jax.random.split(key, 7)
        s = 0.02
        return {'x': jax.random.normal(ks[0], (B, S, D), jnp.float32), 'W_qkv': jax.random.normal(ks[1], (D, 3 * D), jnp.float32) * s, 'b_qkv': jnp.zeros((3 * D,), jnp.float32), 'W_out': jax.random.normal(ks[2], (D, D), jnp.float32) * s, 'b_out': jnp.zeros((D,), jnp.float32), 'rel_emb_k': jax.random.normal(ks[3], (VOCAB, HD), jnp.float32) * s, 'rel_emb_v': jax.random.normal(ks[4], (VOCAB, HD), jnp.float32) * s}
    _L0_attn_in = _L0_attn_setup()

    def _L0_ffn_setup():
        import jax, jax.numpy as jnp
        import numpy as np
        NUM_EXPERTS = 8
        TOP_K = 2
        key = jax.random.key(seed)
        ks = jax.random.split(key, 5)
        B, L, E, H, N = (2, 256, 128, 256, NUM_EXPERTS)
        return {'x': jax.random.normal(ks[0], (B, L, E), dtype=jnp.float32), 'gate_kernel': jax.random.normal(ks[1], (E, N), dtype=jnp.float32) / np.sqrt(E), 'w0_kernel': jax.random.normal(ks[2], (N, E, H), dtype=jnp.float32) / np.sqrt(E), 'w1_kernel': jax.random.normal(ks[3], (N, E, H), dtype=jnp.float32) / np.sqrt(E), 'wo_kernel': jax.random.normal(ks[4], (N, H, E), dtype=jnp.float32) / np.sqrt(H)}
    _L0_ffn_in = _L0_ffn_setup()
    _d = {'L0_attn_x': _L0_attn_in['x'], 'L0_attn_W_qkv': _L0_attn_in['W_qkv'], 'L0_attn_b_qkv': _L0_attn_in['b_qkv'], 'L0_attn_W_out': _L0_attn_in['W_out'], 'L0_attn_b_out': _L0_attn_in['b_out'], 'L0_attn_rel_emb_k': _L0_attn_in['rel_emb_k'], 'L0_attn_rel_emb_v': _L0_attn_in['rel_emb_v'], 'L0_ffn_gate_kernel': _L0_ffn_in['gate_kernel'], 'L0_ffn_w0_kernel': _L0_ffn_in['w0_kernel'], 'L0_ffn_w1_kernel': _L0_ffn_in['w1_kernel'], 'L0_ffn_wo_kernel': _L0_ffn_in['wo_kernel']}
    _x0 = _d['L0_attn_x']
    _d['L0_attn_x'] = jax.random.normal(jax.random.fold_in(jax.random.key(seed), 1), (32, 256, 128), dtype=_x0.dtype)
    del _x0
    return _d

def reference(L0_attn_x, L0_attn_W_qkv, L0_attn_b_qkv, L0_attn_W_out, L0_attn_b_out, L0_attn_rel_emb_k, L0_attn_rel_emb_v, L0_ffn_gate_kernel, L0_ffn_w0_kernel, L0_ffn_w1_kernel, L0_ffn_wo_kernel):

    def _L0_attn_ref(x, W_qkv, b_qkv, W_out, b_out, rel_emb_k, rel_emb_v):
        import jax, jax.numpy as jnp
        import numpy as np
        B, S, D, H, R = (2, 256, 128, 16, 64)
        HD = D // H
        VOCAB = 2 * R + 1
        b, s, d = x.shape
        hd = d // H
        idx = jnp.arange(s)
        dist = jnp.clip(idx[None, :] - idx[:, None], -R, R) + R
        pe_k = rel_emb_k[dist]
        pe_v = rel_emb_v[dist]
        qkv = (x @ W_qkv + b_qkv).reshape(b, s, 3, H, hd)
        qkv = jnp.transpose(qkv, (2, 0, 3, 1, 4))
        q, k, v = (qkv[0], qkv[1], qkv[2])
        q = q / jnp.sqrt(jnp.asarray(hd, x.dtype))
        score = jnp.einsum('bhqd,bhkd->bhqk', q, k) + jnp.einsum('bhqd,qkd->bhqk', q, pe_k)
        attn = jax.nn.softmax(score, axis=-1)
        ctx = jnp.einsum('bhqk,bhkd->bhqd', attn, v) + jnp.einsum('bhqk,qkd->bhqd', attn, pe_v)
        ctx = jnp.transpose(ctx, (0, 2, 1, 3)).reshape(b, s, d)
        return ctx @ W_out + b_out

    def _L0_ffn_ref(x, gate_kernel, w0_kernel, w1_kernel, wo_kernel):
        import jax, jax.numpy as jnp
        import numpy as np
        NUM_EXPERTS = 8
        TOP_K = 2
        B, L, E = x.shape
        gate_logits = jnp.einsum('ble,en->bln', x, gate_kernel)
        top_k_weights, top_k_indices = jax.lax.top_k(gate_logits, TOP_K)
        softmax_probs = jax.nn.softmax(top_k_weights.astype(jnp.float32), axis=-1)
        weights = jnp.zeros_like(gate_logits)
        b_idx = jnp.arange(B)[:, None, None]
        l_idx = jnp.arange(L)[:, None]
        weights = weights.at[b_idx, l_idx, top_k_indices].set(softmax_probs)
        layer_w0 = jnp.einsum('ble,neh->blnh', x, w0_kernel)
        layer_w1 = jnp.einsum('ble,neh->blnh', x, w1_kernel)
        layer_mult = jax.nn.silu(layer_w0) * layer_w1
        intermediate = jnp.einsum('blnh,nhe->blne', layer_mult, wo_kernel)
        output = jnp.einsum('blne,bln->ble', intermediate, weights)
        return output
    x = L0_attn_x
    x = x + _L0_attn_ref(_layernorm(x, axis=-1), L0_attn_W_qkv, L0_attn_b_qkv, L0_attn_W_out, L0_attn_b_out, L0_attn_rel_emb_k, L0_attn_rel_emb_v)
    x = x + _L0_ffn_ref(_layernorm(x, axis=-1), L0_ffn_gate_kernel, L0_ffn_w0_kernel, L0_ffn_w1_kernel, L0_ffn_wo_kernel)
    return x

_drawn_inputs = setup_inputs


def setup_inputs(seed=0):
    import zlib

    import numpy as np

    out = dict(_drawn_inputs(seed))
    spreads = {'L0_attn_b_qkv': (0.0, 0.1), 'L0_attn_b_out': (0.0, 0.1)}
    factors = {'L0_attn_W_qkv': 4.046, 'L0_attn_rel_emb_k': 32.378, 'L0_attn_rel_emb_v': 4.447}
    for name, (base, spread) in spreads.items():
        noise = np.random.default_rng([zlib.crc32(name.encode()), seed]).standard_normal(out[name].shape)
        drawn = base * np.exp(spread * noise) if base else spread * noise
        out[name] = jnp.asarray(drawn.astype(out[name].dtype))
    for name, factor in factors.items():
        out[name] = (out[name] * factor).astype(out[name].dtype)
    return out
```

```python
from contextlib import ExitStack

import numpy as np

import concourse.bass as bass
from concourse import mybir
from concourse.alu_op_type import AluOpType as ALU

F32 = mybir.dt.float32
F32R = mybir.dt.float32r
U32 = mybir.dt.uint32
ACT = mybir.ActivationFunctionType
AX = mybir.AxisListType

P = 128
NB, S, D = 32, 256, 128
H, HD = 16, 8
R = 64
NC = S // P
UH = 8
HU = 4
NU = NB * H // UH
NE, HID = 8, 256
NM = HID // P
BT = 512
NK = NB * S // BT
WIN = R + P
PITCH = WIN + P
VS = 32
EPS = 1e-5
BIG = 3.0e38


def counted(eng, reg, count):
    if isinstance(count.v, int):
        return count.v
    eng.reg_mov(reg, count.v)
    return reg


class Num:

    def __init__(self, v, i):
        self.v, self.i = v, i

    def __mul__(self, k):
        return Num(self.v * k, self.i * k)

    def __add__(self, k):
        return Num(self.v + k, self.i + k)

    def __sub__(self, k):
        return self + (-k)


def layer_program(nc, x, w_qkv, w_out, gate, w0, w1, wo, bqk, bv, bout, ek_win, ek_ref, ev_rows, ev_edge,
                  ident_in, sel_in, pick_in, iota_in, mask_in, out):
    ctx = ExitStack()
    with ctx:
        def sb(name, shape, dt=F32):
            return ctx.enter_context(nc.sbuf_tensor(name, shape, dt))

        def bank(name):
            return ctx.enter_context(nc.psum_tensor(name, [P, 512], F32))

        def sem(name):
            return ctx.enter_context(nc.semaphore(name))

        ident = sb("ident", [P, P])
        sel = sb("sel", [P, 16, P], F32R)
        pick = sb("pick", [16, NE, P], F32R)
        iota = sb("iota", [P, NE])
        mask = sb("mask", [P, 2])
        wqkv_sb = sb("wqkv_sb", [P, 3 * D])
        wout_sb = sb("wout_sb", [P, D])
        gate_sb = sb("gate_sb", [P, NE])
        w0_sb = sb("w0_sb", [P, NE, HID])
        w1_sb = sb("w1_sb", [P, NE, HID])
        wo_sb = sb("wo_sb", [P, NE, NM, D])
        bqk_sb = sb("bqk_sb", [P, 2])
        bv_sb = sb("bv_sb", [P, D])
        bout_sb = sb("bout_sb", [P, D])
        ek_r = sb("ek_r", [P, NC])
        ek_hi = sb("ek_hi", [P, NC, WIN], F32R)
        ek = sb("ek", [P, NC, WIN], F32R)
        ev_r = sb("ev_r", [P, HD])
        edge = sb("edge", [P, 2, D])
        ev = sb("ev", [P, NC, VS])
        ev_tail = sb("ev_tail", [P, NC, D])

        xt = sb("xt", [P, 2, NC, D])
        stat = sb("stat", [P, NC, 6])
        mv = sb("mv", [P, NC, 2])
        mhalf = sb("mhalf", [P, NC])
        vare = sb("vare", [P, NC])
        rstd = sb("rstd", [P, NC])
        xn = sb("xn", [P, NC, D])
        xnT = sb("xnT", [P, S])
        qk32 = sb("qk32", [P, 2, S])
        qk_hi = sb("qk_hi", [P, 2, S], F32R)
        qk_lo = sb("qk_lo", [P, 2, S], F32R)
        qk = sb("qk", [P, 2, 4, 2, S], F32R)
        val = sb("val", [P, 2, NC, H, VS])
        lrow = sb("lrow", [P, 2, NC, HU, WIN])
        bias = sb("bias", [P, NC, UH, S])
        sneg = sb("sneg", [P, 2, NC, S])
        nmax = sb("nmax", [P, 2, NC])
        prob = sb("prob", [P, 2, NC, UH, S])
        prel = sb("prel", [P, NC, UH, WIN])
        tail = sb("tail", [P, 2, NC, H])
        pT = sb("pT", [P, 2, NC, S])
        rT = sb("rT", [P, 2, S])
        cT = sb("cT", [P, 4, S])
        t1 = sb("t1", [P, NC, D])
        t2 = sb("t2", [P, D])
        t3 = sb("t3", [P, NC, D])
        rz = sb("rz", [P, H])
        cn = sb("cn", [P, NC, D])
        cnT = sb("cnT", [P, S])
        xres = sb("xres", [P, NC, D])
        xb = sb("xb", [P, NC, D])
        x1 = sb("x1", [P, NC, D])

        stat2 = sb("stat2", [P, NC, 6])
        mv2 = sb("mv2", [P, NC, 2])
        vare2 = sb("vare2", [P, NC])
        rstd2 = sb("rstd2", [P, NC])
        xn2 = sb("xn2", [P, NC, D])
        lg = sb("lg", [P, NC, NE])
        top = sb("top", [P, NC, 8])
        topi = sb("topi", [P, NC, 8], U32)
        topf = sb("topf", [P, NC, 8])
        gd = sb("gd", [P, NC])
        ge = sb("ge", [P, NC])
        gs = sb("gs", [P, NC])
        gp = sb("gp", [P, 2, NC])
        wa = sb("wa", [P, NC, NE])
        wb = sb("wb", [P, NC, NE])
        wf = sb("wf", [P, NC, NE])
        wr = sb("wr", [P, NC, 2 * NE], F32R)

        xs = sb("xs", [P, BT])
        xw = sb("xw", [P, BT])
        ws = sb("ws", [2 * NE, BT], F32R)
        ww = sb("ww", [2 * NE, BT], F32R)
        xg = sb("xg", [P, 2, BT])
        th = sb("th", [P, BT])
        ug = sb("ug", [P, 2, BT])
        oT = sb("oT", [P, BT])
        xo = sb("xo", [P, 4, D])

        boot = prob[:, 0, :, :, :].rearrange("p c h k -> p (c h k)")
        sel_f = boot[:, 0:16 * P]
        pick_f = boot[0:2 * NE, 16 * P:(16 + NE) * P]
        ek_w = boot[:, (16 + NE) * P:(16 + NE) * P + NC * WIN].rearrange("p (c w) -> p c w", c=NC)

        SB_, LX, PT, RT, PV, H0, H1, OB = (bank(n) for n in ("s_b", "lx_b", "pt_b", "rt_b", "pv_b", "h0_b", "h1_b", "o_b"))

        lscr = nc.dram_tensor("lscr", [2, NC, P, HU, PITCH], F32, kind="Internal").ap()
        pscr = nc.dram_tensor("pscr", [2, NC, P, HU, PITCH], F32, kind="Internal").ap()
        x1d = nc.dram_tensor("x1d", [NB * S, D], F32, kind="Internal").ap()
        CST, IST = P * HU * PITCH, HU * PITCH

        def by_key(half, c):
            return bass.AP(lscr.tensor, (half * NC + c) * CST + P - 1, [[IST - 1, P], [PITCH, HU], [1, WIN]])

        def by_offset(half, c):
            return bass.AP(pscr.tensor, (half * NC + c) * CST + c, [[IST + 1, P], [PITCH, HU], [1, WIN]])

        x_v = x.rearrange("(b c p) d -> b p c d", c=NC, p=P)
        x1_v = x1d.rearrange("(b c p) d -> b p c d", c=NC, p=P)
        x1_kv = x1d.rearrange("(k j p) d -> k p j d", j=4, p=P)
        out_v = out.rearrange("(k j p) d -> k p j d", j=4, p=P)

        s_const, s_const2 = sem("s_const"), sem("s_const2")
        s_zero, s_margin = sem("s_zero"), sem("s_margin")
        s_const_dve, s_boot = sem("s_const_dve"), sem("s_boot")
        s_x = [sem(f"s_xin{i}") for i in range(2)]
        s_mh, s_ve, s_ve2 = sem("s_mh"), sem("s_ve"), sem("s_ve2")
        s_st, s_mv, s_rs = sem("s_st"), sem("s_mv"), sem("s_rs")
        s_xn = sem("s_xn")
        s_xnT_ps, s_xnT = sem("s_xnT_ps"), sem("s_xnT")
        s_qk_ps, s_qk32 = sem("s_qk_ps"), sem("s_qk32")
        s_hi, s_lo = sem("s_hi"), sem("s_lo")
        s_stk_ps, s_stk = sem("s_stk_ps"), sem("s_stk")
        s_v_ps, s_v = sem("s_v_ps"), sem("s_v")
        s_l_ps, s_l = sem("s_l_ps"), sem("s_l")
        s_lw = [sem(f"s_lw{i}") for i in range(2)]
        s_br = [sem(f"s_br{i}") for i in range(2)]
        s_s, s_ttr = sem("s_s"), sem("s_ttr")
        s_exp = sem("s_exp")
        s_pw = [sem(f"s_pw{i}") for i in range(2)]
        s_pr = [sem(f"s_pr{i}") for i in range(2)]
        s_tail = sem("s_tail")
        s_pt_ps, s_pt = sem("s_pt_ps"), sem("s_pt")
        s_rt_ps, s_rt = sem("s_rt_ps"), sem("s_rt")
        s_pv, s_cT = sem("s_pv"), sem("s_cT")
        s_cx_ps = sem("s_cx_ps")
        s_t1, s_rz, s_t2, s_t3, s_cn = (sem(n) for n in ("s_t1", "s_rz", "s_t2", "s_t3", "s_cn"))
        s_cnT_ps, s_cnT = sem("s_cnT_ps"), sem("s_cnT")
        s_xr, s_xb = sem("s_xr"), sem("s_xb")
        s_op_ps, s_x1, s_x1w = sem("s_op_ps"), sem("s_x1"), sem("s_x1w")
        s_st2, s_mv2, s_rs2, s_xn2 = sem("s_st2"), sem("s_mv2"), sem("s_rs2"), sem("s_xn2")
        s_xs_ps, s_xs = sem("s_xs_ps"), sem("s_xs")
        s_g_ps, s_lg = sem("s_g_ps"), sem("s_lg")
        s_top, s_topi, s_topf, s_gd, s_ge = sem("s_top"), sem("s_topi"), sem("s_topf"), sem("s_gd"), sem("s_ge")
        s_gs, s_gp1, s_gp2, s_oh, s_wf, s_wh, s_wl = (sem(n) for n in ("s_gs", "s_gp1", "s_gp2", "s_oh", "s_wf", "s_wh", "s_wl"))
        s_ws_ps, s_ws = sem("s_ws_ps"), sem("s_ws")
        s_ww, s_xw = sem("s_ww"), sem("s_xw")
        s_wb_ps, s_xg = sem("s_wb_ps"), sem("s_xg")
        s_h0, s_h1, s_th, s_ag, s_ug, s_wo = (sem(n) for n in ("s_h0", "s_h1", "s_th", "s_ag", "s_ug", "s_wo"))
        s_oT, s_f_ps, s_fin, s_xo, s_out = sem("s_oT"), sem("s_f_ps"), sem("s_fin"), sem("s_xo"), sem("s_out")

        LOOP = (3, 15)
        LAST = NK + 2

        def iterations(eng, body):
            for i in range(LOOP[0]):
                body(Num(i, i))
            with eng.Fori(*LOOP) as t:
                body(Num(t, LOOP[0] + 1))
            for i in range(LOOP[1], LAST + 1):
                body(Num(i, i))

        block = ctx.enter_context(nc.Block())

        @block.sync
        def _(sp):
            counts = [sp.alloc_register(f"sp_count{i}") for i in range(3)]
            for dst, src in ((ident[:, :], ident_in), (iota[:, :], iota_in), (mask[:, :], mask_in),
                             (wqkv_sb[:, :], w_qkv), (bqk_sb[:, :], bqk), (bv_sb[:, :], bv),
                             (sel_f, sel_in.rearrange("p g m -> p (g m)")), (ek_w, ek_win), (ek_r[:, :], ek_ref), (ev_r[:, :], ev_rows),
                             (edge[:, :, :], ev_edge), (pick_f, pick_in.rearrange("p e m -> p (e m)"))):
                sp.dma_start(dst, src).then_inc(s_const, 16)
            sp.dma_start(xt[:, 0, :, :], x_v[0]).then_inc(s_x[0], 16)
            sp.dma_start(xt[:, 1, :, :], x_v[1]).then_inc(s_x[1], 16)
            sp.wait_ge(s_zero, 1)
            zv = sneg[:, 0, :, :].rearrange("p c (h m) -> p (c h) m", h=2)
            for half in range(2):
                for scr, (m0, m1) in ((lscr, (WIN, 0)), (pscr, (0, WIN))):
                    sp.dma_start(scr[half, 0, :, :, m0:m0 + P], zv).then_inc(s_margin, 16)
                    sp.dma_start(scr[half, 1, :, :, m1:m1 + P], zv).then_inc(s_margin, 16)
            for dst, src in ((wout_sb[:, :], w_out), (bout_sb[:, :], bout), (gate_sb[:, :], gate),
                             (w0_sb[:, :, :], w0.rearrange("n e h -> e n h")),
                             (w1_sb[:, :, :], w1.rearrange("n e h -> e n h")),
                             (wo_sb[:, :, :, :], wo.rearrange("n (m p) e -> p n m e", p=P))):
                sp.dma_start(dst, src).then_inc(s_const2, 16)
            sp.wait_ge(s_margin, 16 * 8)

            def store_l(u, half):
                ready0 = counted(sp, counts[0], u * UH + HU * (half + 1))
                if u.i >= 1:
                    ready1 = counted(sp, counts[1], u * 32)
                sp.wait_ge(s_margin, 16 * 8)
                sp.wait_ge(s_l, ready0)
                if u.i >= 1:
                    sp.wait_ge(s_br[half], ready1)
                for c, at in ((0, 0), (1, P)):
                    sp.dma_start(lscr[half, c, :, :, at:at + WIN], lrow[:, half, c, :, :]).then_inc(s_lw[half], 16)

            def load_bias(u, half):
                ready0 = counted(sp, counts[0], u * 32 + 32)
                if u.i >= 1:
                    ready1 = counted(sp, counts[1], (u - 1) * 16 + 8 * (half + 1))
                sp.wait_ge(s_margin, 16 * 8)
                sp.wait_ge(s_lw[half], ready0)
                if u.i >= 1:
                    sp.wait_ge(s_ttr, ready1)
                heads = slice(HU * half, HU * half + HU)
                for c in range(NC):
                    sp.dma_start(bias[:, c, heads, R * c:R * c + WIN], by_key(half, c)).then_inc(s_br[half], 16)

            def store_p(u, half, par):
                ready0 = counted(sp, counts[0], u * 16 + 8 * (half + 1))
                if u.i >= 1:
                    ready1 = counted(sp, counts[1], u * 32)
                sp.wait_ge(s_margin, 16 * 8)
                sp.wait_ge(s_exp, ready0)
                if u.i >= 1:
                    sp.wait_ge(s_pr[half], ready1)
                heads = slice(HU * half, HU * half + HU)
                for c, at in ((0, P - 1), (1, 0)):
                    sp.dma_start(pscr[half, c, :, :, at:at + WIN],
                                 prob[:, par, c, heads, R * c:R * c + WIN]).then_inc(s_pw[half], 16)

            def load_prel(u, half):
                ready0 = counted(sp, counts[0], u * 32 + 32)
                if u.i >= 1:
                    ready1 = counted(sp, counts[1], (u - 1) * UH + HU * (half + 1))
                    ready2 = counted(sp, counts[2], (u - 1) * 4 + 2 * (half + 1))
                sp.wait_ge(s_margin, 16 * 8)
                sp.wait_ge(s_pw[half], ready0)
                if u.i >= 1:
                    sp.wait_ge(s_rt_ps, ready1)
                    sp.wait_ge(s_tail, ready2)
                heads = slice(HU * half, HU * half + HU)
                for c in range(NC):
                    sp.dma_start(prel[:, c, heads, :], by_offset(half, c)).then_inc(s_pr[half], 16)

            for half in range(2):
                store_l(Num(0, 0), half)
                load_bias(Num(0, 0), half)

            def body(t):
                for s in range(4):
                    u = t * 4 + s
                    for n in range(UH):
                        if n in (0, 4):
                            half = 1 if n == 0 else 0
                            pu, lu = (u - 1, u) if n == 0 else (u, u + 1)
                            if 0 <= pu.i < NU:
                                store_p(pu, half, (s + 1) % 2 if n == 0 else s % 2)
                            if 1 <= lu.i < NU:
                                store_l(lu, half)
                            if 0 <= pu.i < NU:
                                load_prel(pu, half)
                            if 1 <= lu.i < NU:
                                load_bias(lu, half)
                        if s % 2 == 0:
                            b = t * 2 + s // 2
                            if n == 3 and b.i + 2 < NB:
                                ready = counted(sp, counts[0], b * 2 + 2)
                                sp.wait_ge(s_margin, 16 * 8)
                                sp.wait_ge(s_xn, ready)
                                sp.dma_start(xt[:, (s // 2) % 2, :, :], x_v[(b + 2).v]).then_inc(s_x[(s // 2) % 2], 16)
                            if n == 2 and 0 <= b.i - 2 < NB:
                                pb = b - 2
                                ready = counted(sp, counts[0], pb + 1)
                                sp.wait_ge(s_margin, 16 * 8)
                                sp.wait_ge(s_x1, ready)
                                sp.dma_start(x1_v[pb.v], x1[:, :, :]).then_inc(s_x1w, 16)
                        else:
                            b = t * 2 + (s - 3) // 2
                            if n == 2 and 0 <= b.i < NB:
                                if b.i >= 1:
                                    ready = counted(sp, counts[0], b * 1)
                                sp.wait_ge(s_margin, 16 * 8)
                                if b.i >= 1:
                                    sp.wait_ge(s_xb, ready)
                                sp.dma_start(xres[:, :, :], x_v[b.v]).then_inc(s_xr, 16)
                        k = t - 3
                        if s == 1 and 0 <= k.i < NK:
                            if n == 1:
                                ready0 = counted(sp, counts[0], k * 32 + 32)
                                if k.i >= 1:
                                    ready1 = counted(sp, counts[1], k * 16)
                                sp.wait_ge(s_margin, 16 * 8)
                                sp.wait_ge(s_x1w, ready0)
                                if k.i >= 1:
                                    sp.wait_ge(s_out, ready1)
                                sp.dma_start(xo[:, :, :], x1_kv[k.v]).then_inc(s_xo, 16)
                            if n == 7:
                                ready = counted(sp, counts[0], k + 1)
                                sp.wait_ge(s_margin, 16 * 8)
                                sp.wait_ge(s_fin, ready)
                                sp.dma_start(out_v[k.v], xo[:, :, :]).then_inc(s_out, 16)

            iterations(sp, body)
            sp.wait_ge(s_x1w, 16 * NB)
            sp.wait_ge(s_out, 16 * NK)

        @block.gpsimd
        def _(gp_):
            counts = [gp_.alloc_register(f"gp__count{i}") for i in range(3)]
            gp_.memset(sneg[:, 0, :, :], 0.0).then_inc(s_zero, 1)

            def normalise(b, par):
                if b.i >= 1:
                    ready0 = counted(gp_, counts[0], b * 1)
                ready1 = counted(gp_, counts[1], b * 2 + 2)
                gp_.wait_ge(s_zero, 1)
                if b.i >= 1:
                    gp_.wait_ge(s_xnT_ps, ready0)
                gp_.wait_ge(s_mv, ready1)
                gp_.tensor_scalar(vare[:, :], mv[:, :, 1], EPS, None, ALU.add).then_inc(s_ve, 1)
                gp_.wait_ge(s_ve, (b + 1).v)
                gp_.tensor_tensor(rstd[:, :], vare[:, :], mhalf[:, :], ALU.pow).then_inc(s_rs, 1)
                ready = counted(gp_, counts[0], b + 1)
                gp_.wait_ge(s_zero, 1)
                gp_.wait_ge(s_rs, ready)
                for c in range(NC):
                    gp_.tensor_scalar(xn[:, c, :], xt[:, par, c, :], mv[:, c, 0:1], rstd[:, c:c + 1],
                                      ALU.subtract, ALU.mult).then_inc(s_xn, 1)

            gp_.memset(mhalf[:, :], -0.5).then_inc(s_mh, 1)
            gp_.wait_ge(s_mh, 1)
            normalise(Num(0, 0), 0)
            gp_.wait_ge(s_boot, 1)

            def body(t):
                for s in range(4):
                    for n in range(UH):
                        if s % 2 == 0:
                            b = t * 2 + s // 2 + 1
                            if n == 0 and b.i < NB:
                                normalise(b, (s // 2 + 1) % 2)
                            pb = t * 2 + s // 2 - 2
                            if n == 1 and 0 <= pb.i < NB:
                                if pb.i >= 1:
                                    ready0 = counted(gp_, counts[0], pb * 1)
                                ready1 = counted(gp_, counts[1], pb * 2 + 2)
                                gp_.wait_ge(s_zero, 1)
                                if pb.i >= 1:
                                    gp_.wait_ge(s_xs_ps, ready0)
                                gp_.wait_ge(s_mv2, ready1)
                                gp_.tensor_scalar(vare2[:, :], mv2[:, :, 1], EPS, None, ALU.add).then_inc(s_ve2, 1)
                                gp_.wait_ge(s_ve2, (pb + 1).v)
                                gp_.tensor_tensor(rstd2[:, :], vare2[:, :], mhalf[:, :], ALU.pow).then_inc(s_rs2, 1)
                                ready = counted(gp_, counts[0], pb + 1)
                                gp_.wait_ge(s_zero, 1)
                                gp_.wait_ge(s_rs2, ready)
                                for c in range(NC):
                                    gp_.tensor_scalar(xn2[:, c, :], x1[:, c, :], mv2[:, c, 0:1], rstd2[:, c:c + 1],
                                                      ALU.subtract, ALU.mult).then_inc(s_xn2, 1)
                        else:
                            pb = t * 2 + (s - 3) // 2
                            par = ((s - 3) // 2) % 2
                            if 0 <= pb.i < NB:
                                if n == 2:
                                    gp_.wait_ge(s_tail, (pb * 8 + 8).v)
                                    if pb.i >= 1:
                                        gp_.wait_ge(s_t2, (pb * 2).v)
                                    for c in range(NC):
                                        gp_.tensor_tensor(t1[:, c, :].rearrange("p (h d) -> p h d", d=HD),
                                                          tail[:, par, c, :].unsqueeze(2).to_broadcast([P, H, HD]),
                                                          ev_tail[:, c, :].rearrange("p (h d) -> p h d", d=HD),
                                                          ALU.mult).then_inc(s_t1, 1)
                                if n in (4, 5):
                                    c = n - 4
                                    gp_.wait_ge(s_t3, (pb * 2 + c + 1).v)
                                    if c == 0 and pb.i >= 1:
                                        gp_.wait_ge(s_cnT_ps, (pb * 1).v)
                                    gp_.tensor_tensor(cn[:, c, :], t3[:, c, :], edge[:, 1 - c, :],
                                                      ALU.add).then_inc(s_cn, 1)
                                if n == 6:
                                    gp_.wait_ge(s_xr, (pb * 16 + 16).v)
                                    if pb.i == 0:
                                        gp_.wait_ge(s_const2, 16 * 6)
                                    if pb.i >= 1:
                                        gp_.wait_ge(s_x1, (pb * 1).v)
                                    gp_.tensor_tensor(xb[:, :, :], xres[:, :, :],
                                                      bout_sb[:, :].unsqueeze(1).to_broadcast([P, NC, D]),
                                                      ALU.add).then_inc(s_xb, 1)
                        k = t - 1
                        if s == 3 and n == 3 and 0 <= k.i < NK:
                            ready0 = counted(gp_, counts[0], k * 2 + 2)
                            if k.i >= 1:
                                ready1 = counted(gp_, counts[1], k * NE)
                            gp_.wait_ge(s_zero, 1)
                            gp_.wait_ge(s_ws, ready0)
                            if k.i >= 1:
                                gp_.wait_ge(s_wb_ps, ready1)
                            gp_.tensor_copy(ww[:, :], ws[:, :]).then_inc(s_ww, 1)
                        if s == 3 and n == 7 and 0 <= k.i < NK:
                            ready0 = counted(gp_, counts[0], k * 2 + 2)
                            if k.i >= 1:
                                ready1 = counted(gp_, counts[1], k * NE * NM)
                            gp_.wait_ge(s_zero, 1)
                            gp_.wait_ge(s_xs, ready0)
                            if k.i >= 1:
                                gp_.wait_ge(s_h0, ready1)
                            gp_.tensor_copy(xw[:, :], xs[:, :]).then_inc(s_xw, 1)

            iterations(gp_, body)

        @block.tensor
        def _(pe):
            mm, tr = nc.tensor.matmul, nc.tensor.transpose
            lx = [None]

            def lx_free():
                if lx[0] is not None and lx[0][1].i > 0:
                    pe.wait_ge(lx[0][0], lx[0][1].v)

            def rows_T(b):
                lx_free()
                pe.wait_ge(s_xn, (b * 2 + 2).v)
                for c in range(NC):
                    last = tr(LX[:, P * c:P * c + P], xn[:, c, :], ident[:, :])
                last.then_inc(s_xnT_ps, 1)
                lx[0] = (s_xnT, b + 1)

            def project(b):
                lx_free()
                pe.wait_ge(s_xnT, (b + 1).v)
                for w in range(2):
                    last = mm(LX[:, S * w:S * w + S], wqkv_sb[:, D * w:D * w + D], xnT[:, :], start=True, stop=True)
                last.then_inc(s_qk_ps, 1)
                lx[0] = (s_qk32, b * 2 + 2)

            def stack(b, g):
                lx_free()
                pe.wait_ge(s_hi, (b + 1).v)
                pe.wait_ge(s_lo, (b + 1).v)
                for w in range(2):
                    mm(LX[:, S * w:S * w + S], sel[:, 4 * g + 2 * w, :], qk_hi[:, w, :], start=True, stop=False)
                    last = mm(LX[:, S * w:S * w + S], sel[:, 4 * g + 2 * w + 1, :], qk_lo[:, w, :],
                              start=False, stop=True)
                last.then_inc(s_stk_ps, 1)
                lx[0] = (s_stk, b * 4 + g + 1)

            def values(b):
                lx_free()
                for c in range(NC):
                    last = mm(LX[:, D * c:D * c + D], xnT[:, P * c:P * c + P], wqkv_sb[:, 2 * D:3 * D],
                              start=True, stop=True)
                last.then_inc(s_v_ps, 1)
                lx[0] = (s_v, b + 1)

            def rel_logits(u, par, half, n):
                g, j = 2 * half + n // 4, n % 4
                lx_free()
                if n % 4 == 0:
                    pe.wait_ge(s_stk, (u * 2 + n // 4 + 1).v)
                rows = slice(32 * j, 32 * j + 32)
                for c in range(NC):
                    last = mm(LX[:, WIN * c:WIN * c + WIN], qk[rows, par, g, 0, P * c:P * c + P], ek[rows, c, :],
                              start=True, stop=True)
                last.then_inc(s_l_ps, 1)
                lx[0] = (s_l, u * UH + n + 1)

            def scores(u, par, half, n):
                g, j = 2 * half + n // 4, n % 4
                if u.i > 0 or n > 0:
                    pe.wait_ge(s_ttr, (u * 16 + 2 * n).v)
                rows = slice(32 * j, 32 * j + 32)
                for c in range(NC):
                    last = mm(SB_[:, S * c:S * c + S], qk[rows, par, g, 0, P * c:P * c + P], qk[rows, par, g, 1, :],
                              start=True, stop=True)
                last.then_inc(s_s, 1)

            def transposes(u, upar, n):
                if n == 0:
                    pe.wait_ge(s_exp, (u * 16 + 16).v)
                if u.i > 0 or n > 0:
                    pe.wait_ge(s_pt, (u * UH + n).v)
                for kc in range(NC):
                    for c in range(NC):
                        last = tr(PT[:, S * kc + P * c:S * kc + P * c + P], prob[:, upar, c, n, P * kc:P * kc + P],
                                  ident[:, :])
                last.then_inc(s_pt_ps, 1)

            def band_transposes(u, n, spread):
                if u.i > 0 or n > 0:
                    pe.wait_ge(s_rt, (u * UH + n).v)
                if spread is not None and spread.i > 0:
                    pe.wait_ge(s_xg, spread.v)
                if n % 4 == 0:
                    pe.wait_ge(s_pr[n // 4], (u * 32 + 32).v)
                for c, at in ((0, R), (1, 0)):
                    last = tr(RT[:, P * c:P * c + P], prel[:, c, n, at:at + P], ident[:, :])
                last.then_inc(s_rt_ps, 1)

            def context(u, batches, par, half, n):
                h, j, hp = UH * half + n, n % 4, n % 2
                o = PV[32 * j:32 * j + 32, S * (n // 4):S * (n // 4) + S]
                if n == 0:
                    pe.wait_ge(s_v, batches.v)
                    if u.i > 0:
                        pe.wait_ge(s_cT, (u * 1).v)
                pe.wait_ge(s_pt, (u * UH + n + 1).v)
                pe.wait_ge(s_rt, (u * UH + n + 1).v)
                mm(o, val[:, par, 0, h, :], pT[:, hp, 0, :], start=True, stop=False)
                mm(o, val[:, par, 1, h, :], pT[:, hp, 1, :], start=False, stop=False)
                for c in range(NC):
                    last = mm(o[:, P * c:P * c + P], ev[:, c, :], rT[:, hp, P * c:P * c + P],
                              start=False, stop=(c == 1))
                last.then_inc(s_pv, 1)

            pe.wait_ge(s_const, 16 * 12)
            rows_T(Num(0, 0))
            project(Num(0, 0))
            pe.wait_ge(s_boot, 1)
            for g in range(4):
                stack(Num(0, 0), g)
            values(Num(0, 0))
            for n in range(UH):
                rel_logits(Num(0, 0), 0, 0, n)

            def body(t):
                lx[0] = None
                if t.i > 0:
                    pe.wait_ge(s_l, (t * 32 + 8).v if t.i < NK else NU * UH)
                    if 0 <= (t * 2 - 2).i < NB:
                        pe.wait_ge(s_cnT, (t * 2 - 1).v)
                else:
                    pe.wait_ge(s_l, UH)
                rt_spread = None
                for s in range(4):
                    u = t * 4 + s
                    half = s % 2
                    for n in range(UH):
                        q = s * UH + n
                        if u.i < NU:
                            scores(u, (s // 2) % 2, half, n)
                        if u.i + 1 < NU:
                            rel_logits(u + 1, ((s + 1) // 2) % 2, (s + 1) % 2, n)
                        v = u - 1
                        if 0 <= v.i < NU:
                            batches = t * 2 + (s + 1) // 2
                            transposes(v, (s + 1) % 2, n)
                            band_transposes(v, n, rt_spread)
                            rt_spread = None
                            if n > 0:
                                context(v, batches, ((s - 1) // 2) % 2, (s + 1) % 2, n - 1)
                        if s % 2 == 0:
                            b = t * 2 + s // 2 + 1
                            if b.i < NB:
                                if n == 1:
                                    rows_T(b)
                                if n == 3:
                                    project(b)
                                if n in (5, 6):
                                    stack(b, n - 5)
                        else:
                            b = t * 2 + (s - 1) // 2 + 1
                            if b.i < NB:
                                if n in (0, 1):
                                    stack(b, n + 2)
                                if n == 2:
                                    values(b)
                        if s % 2 == 1:
                            pb = t * 2 + (s - 3) // 2
                            if 0 <= pb.i < NB:
                                if n in (3, 4):
                                    c = n - 3
                                    lx_free()
                                    pe.wait_ge(s_cT, (pb * 2 + 2).v)
                                    for g in range(4):
                                        last = tr(LX[:, P * g:P * g + P], cT[:, g, P * c:P * c + P], ident[:, :])
                                    last.then_inc(s_cx_ps, 1)
                                    lx[0] = (s_t2, pb * 2 + c + 1)
                                if n == 6:
                                    lx_free()
                                    pe.wait_ge(s_cn, (pb * 2 + 2).v)
                                    for c in range(NC):
                                        last = tr(LX[:, P * c:P * c + P], cn[:, c, :], ident[:, :])
                                    last.then_inc(s_cnT_ps, 1)
                                    lx[0] = (s_cnT, pb + 1)
                        else:
                            pb = t * 2 + s // 2 - 2
                            if 0 <= pb.i < NB:
                                if n == 0:
                                    lx_free()
                                    if pb.i == 0:
                                        pe.wait_ge(s_const2, 16 * 6)
                                    pe.wait_ge(s_cnT, (pb + 1).v)
                                    for c in range(NC):
                                        last = mm(LX[:, P * c:P * c + P], cnT[:, P * c:P * c + P], wout_sb[:, :],
                                                  start=True, stop=True)
                                    last.then_inc(s_op_ps, 1)
                                    lx[0] = (s_x1, pb + 1)
                                if n == 2:
                                    lx_free()
                                    pe.wait_ge(s_xn2, (pb * 2 + 2).v)
                                    for c in range(NC):
                                        last = tr(LX[:, P * c:P * c + P], xn2[:, c, :], ident[:, :])
                                    last.then_inc(s_xs_ps, 1)
                                    lx[0] = (s_xs, pb + 1)
                                if n == 4:
                                    lx_free()
                                    pe.wait_ge(s_xs, (pb + 1).v)
                                    o = BT // 2 * ((s // 2) % 2)
                                    for c in range(NC):
                                        last = mm(LX[:, NE * c:NE * c + NE], xs[:, o + P * c:o + P * c + P],
                                                  gate_sb[:, :], start=True, stop=True)
                                    last.then_inc(s_g_ps, 1)
                                    lx[0] = (s_lg, pb + 1)
                                if n == 7:
                                    lx_free()
                                    pe.wait_ge(s_wl, (pb + 1).v)
                                    for c in range(NC):
                                        last = tr(LX[0:2 * NE, P * c:P * c + P], wr[:, c, :].bitcast(F32), ident[:, :])
                                    last.then_inc(s_ws_ps, 1)
                                    lx[0] = (s_ws, pb + 1)
                        k = t - 2
                        if 0 <= k.i < NK:
                            p, e, m = q // 2, q // 4, (q // 2) % 2
                            kp = k * (NE * NM) + p
                            if q % 2 == 0:
                                if p == 0:
                                    pe.wait_ge(s_xw, (k + 1).v)
                                    if k.i == 0:
                                        pe.wait_ge(s_const2, 16 * 6)
                                if kp.i > 0:
                                    pe.wait_ge(s_ug, (kp * 1).v)
                                mm(H0[:, :], w0_sb[:, e, P * m:P * m + P], xw[:, :],
                                   start=True, stop=True).then_inc(s_h0, 1)
                                pe.wait_ge(s_xg, (k * NE + e + 1).v)
                                mm(H1[:, :], w1_sb[:, e, P * m:P * m + P], xg[:, e % 2, :],
                                   start=True, stop=True).then_inc(s_h1, 1)
                            else:
                                pe.wait_ge(s_ug, (kp + 1).v)
                                if p == 0 and k.i > 0:
                                    pe.wait_ge(s_oT, (k * 1).v)
                                mm(OB[:, :], wo_sb[:, e, m, :], ug[:, p % 2, :],
                                   start=(p == 0), stop=(p == NE * NM - 1)).then_inc(s_wo, 1)
                        for kk, ee in ([(k, q // 4 + 1)] if q % 4 == 1 and q < 28 else [(k + 1, 0)] if q == 29 else []):
                            if 0 <= kk.i < NK:
                                x_e = kk * NE + ee
                                if u.i - 1 < NU and u.i >= 1:
                                    pe.wait_ge(s_rt, ((u - 1) * UH + n + 1).v)
                                if x_e.i > 0:
                                    pe.wait_ge(s_xg, (x_e * 1).v)
                                if ee == 0:
                                    pe.wait_ge(s_ww, (kk + 1).v)
                                mm(RT[:, :], pick[:, ee, :], ww[:, :], start=True, stop=True).then_inc(s_wb_ps, 1)
                                rt_spread = x_e + 1
                        if 0 <= v.i < NU and n == UH - 1:
                            context(v, batches, ((s - 1) // 2) % 2, (s + 1) % 2, n)
                        kf = t - 3
                        if s == 1 and n == 5 and 0 <= kf.i < NK:
                            lx_free()
                            pe.wait_ge(s_oT, (kf + 1).v)
                            for i in range(4):
                                last = tr(LX[:, P * i:P * i + P], oT[:, P * i:P * i + P], ident[:, :])
                            last.then_inc(s_f_ps, 1)
                            lx[0] = (s_fin, kf + 1)

            iterations(pe, body)

        @block.scalar
        def _(act):
            f = nc.scalar.activation

            def take_xnT(b):
                act.wait_ge(s_xnT_ps, (b + 1).v)
                if b.i >= 1:
                    act.wait_ge(s_v_ps, (b * 1).v)
                f(xnT[:, :], LX[:, 0:S], ACT.Copy).then_inc(s_xnT, 1)

            def hi_parts(b):
                act.wait_ge(s_qk32, (b * 2 + 2).v)
                if b.i >= 1:
                    act.wait_ge(s_stk_ps, (b * 4).v)
                f(qk_hi[:, :, :], qk32[:, :, :], ACT.Copy).then_inc(s_hi, 1)

            def take_stack(b, par, g):
                act.wait_ge(s_stk_ps, (b * 4 + g + 1).v)
                f(qk[:, par, g, :, :], LX[:, :].rearrange("p (w s) -> p w s", w=2), ACT.Copy).then_inc(s_stk, 1)

            take_xnT(Num(0, 0))
            hi_parts(Num(0, 0))
            act.wait_ge(s_boot, 1)
            for g in range(4):
                take_stack(Num(0, 0), 0, g)

            def body(t):
                for s in range(4):
                    u = t * 4 + s
                    for n in range(UH):
                        q = s * UH + n
                        k = t - 2
                        if q == 0 and 0 <= t.i - 3 < NK:
                            act.wait_ge(s_wo, ((t - 3) * 16 + 16).v)
                            if t.i > 3:
                                act.wait_ge(s_f_ps, (t - 3).v)
                            f(oT[:, :], OB[:, :], ACT.Copy).then_inc(s_oT, 1)
                        if q % 2 == 1 and 0 <= k.i < NK:
                            kp = k * 16 + q // 2
                            act.wait_ge(s_h0, (kp + 1).v)
                            if kp.i > 0:
                                act.wait_ge(s_ug, (kp * 1).v)
                            f(th[:, :], H0[:, :], ACT.Tanh, scale=0.5).then_inc(s_th, 1)
                        v = u - 1
                        if 0 <= v.i < NU:
                            hp = n % 2
                            act.wait_ge(s_pt_ps, (v * UH + n + 1).v)
                            if v.i > 0 or n > 1:
                                act.wait_ge(s_pv, (v * UH + n - 1).v)
                            f(pT[:, hp, :, :], PT[:, :].rearrange("p (c s) -> p c s", c=NC), ACT.Copy).then_inc(s_pt, 1)
                            act.wait_ge(s_rt_ps, (v * UH + n + 1).v)
                            f(rT[:, hp, :], RT[:, 0:S], ACT.Copy).then_inc(s_rt, 1)
                        if u.i < NU:
                            if n == 0 and u.i >= 2:
                                act.wait_ge(s_pt_ps, ((u - 1) * UH).v)
                                for half in range(2):
                                    act.wait_ge(s_pw[half], ((u - 1) * 32).v)
                            for c in range(NC):
                                act.wait_ge(s_ttr, (u * 16 + 2 * n + c + 1).v)
                                f(prob[:, s % 2, c, n, :], sneg[:, n % 2, c, :], ACT.Exp,
                                  bias=nmax[:, n % 2, c:c + 1], scale=-1.0).then_inc(s_exp, 1)
                        if 0 <= v.i < NU and n == UH - 1:
                            act.wait_ge(s_pv, (v * UH + UH).v)
                            if s % 2 == 1 and v.i >= 2:
                                act.wait_ge(s_cx_ps, ((t * 2 + (s - 3) // 2) * 2 + 2).v)
                            g = 2 * ((s + 1) % 2)
                            f(cT[:, g:g + 2, :], PV[:, :].rearrange("p (g s) -> p g s", g=2), ACT.Copy).then_inc(s_cT, 1)
                        if s % 2 == 0:
                            b = t * 2 + s // 2 + 1
                            par = (s // 2 + 1) % 2
                            if b.i < NB:
                                if n == 1:
                                    take_xnT(b)
                                if n == 4:
                                    hi_parts(b)
                                if n == 5:
                                    take_stack(b, par, 0)
                            pb = t * 2 + s // 2 - 2
                            if 0 <= pb.i < NB:
                                o = BT // 2 * ((s // 2) % 2)
                                if n == 2:
                                    act.wait_ge(s_xs_ps, (pb + 1).v)
                                    if pb.i >= 2:
                                        act.wait_ge(s_xw, ((t - 2) + 1).v)
                                        act.wait_ge(s_xg, ((t - 2) * NE + 1).v)
                                    f(xs[:, o:o + S], LX[:, 0:S], ACT.Copy).then_inc(s_xs, 1)
                                if n == 5:
                                    act.wait_ge(s_gd, (pb + 1).v)
                                    f(ge[:, :], gd[:, :], ACT.Exp).then_inc(s_ge, 1)
                                if n == 7:
                                    act.wait_ge(s_ws_ps, (pb + 1).v)
                                    if pb.i >= 2:
                                        act.wait_ge(s_ww, ((t - 2) + 1).v)
                                    f(ws[:, o:o + S], LX[0:2 * NE, 0:S], ACT.Copy).then_inc(s_ws, 1)
                        else:
                            b = t * 2 + (s - 1) // 2 + 1
                            par = ((s - 1) // 2 + 1) % 2
                            if b.i < NB and n == 0:
                                take_stack(b, par, 2)
                            pb = t * 2 + (s - 3) // 2
                            if 0 <= pb.i < NB and n == 6:
                                act.wait_ge(s_cnT_ps, (pb + 1).v)
                                if pb.i >= 1:
                                    act.wait_ge(s_op_ps, (pb * 1).v)
                                f(cnT[:, :], LX[:, 0:S], ACT.Copy).then_inc(s_cnT, 1)

            iterations(act, body)

        @block.vector
        def _(dve):
            counts = [dve.alloc_register(f"dve_count{i}") for i in range(3)]
            V = nc.vector

            def stats(b, loads, par):
                dve.wait_ge(s_x[par], (loads * 16).v)
                if b.i >= 1:
                    dve.wait_ge(s_xn, (b * 2).v)
                for c in range(NC):
                    V.bn_stats(stat[:, c, :], xt[:, par, c, :]).then_inc(s_st, 1)
                for c in range(NC):
                    ready = counted(dve, counts[0], b * 2 + c + 1)
                    dve.wait_ge(s_const, 16 * 12)
                    dve.wait_ge(s_st, ready)
                    V.bn_aggr(mv[:, c, :], stat[:, c, :]).then_inc(s_mv, 1)

            def take_qk(b):
                dve.wait_ge(s_qk_ps, (b + 1).v)
                if b.i >= 1:
                    dve.wait_ge(s_lo, (b * 1).v)
                    dve.wait_ge(s_hi, (b * 1).v)
                V.tensor_scalar(qk32[:, 0, :], LX[:, 0:S], bqk_sb[:, 0:1], float(HD) ** -0.5,
                                ALU.add, ALU.mult).then_inc(s_qk32, 1)
                V.tensor_scalar(qk32[:, 1, :], LX[:, S:2 * S], bqk_sb[:, 1:2], None, ALU.add).then_inc(s_qk32, 1)

            def lo_parts(b):
                dve.wait_ge(s_hi, (b + 1).v)
                if b.i >= 1:
                    dve.wait_ge(s_stk_ps, (b * 4).v)
                V.tensor_tensor(qk_lo[:, :, :], qk32[:, :, :], qk_hi[:, :, :].bitcast(F32),
                                ALU.subtract).then_inc(s_lo, 1)

            def take_stack(b, par, g):
                dve.wait_ge(s_stk_ps, (b * 4 + g + 1).v)
                V.tensor_copy(qk[:, par, g, :, :], LX[:, :].rearrange("p (w s) -> p w s", w=2)).then_inc(s_stk, 1)

            def take_values(b, par):
                dve.wait_ge(s_v_ps, (b + 1).v)
                if b.i >= 2:
                    dve.wait_ge(s_pv, ((b - 1) * 16).v)
                V.tensor_tensor(val[:, par, :, :, 0:HD],
                                LX[:, 0:2 * D].rearrange("p (c h d) -> p c h d", c=NC, d=HD),
                                bv_sb[:, :].rearrange("p (h d) -> p h d", d=HD).unsqueeze(1).to_broadcast([P, NC, H, HD]),
                                ALU.add).then_inc(s_v, 1)

            def take_l(u, n):
                dve.wait_ge(s_l_ps, (u * UH + n + 1).v)
                if n % 4 == 0 and u.i >= 1:
                    dve.wait_ge(s_lw[n // 4], (u * 32).v)
                V.tensor_copy(lrow[:, n // 4, :, n % 4, :],
                              LX[:, 0:2 * WIN].rearrange("p (c w) -> p c w", c=NC)).then_inc(s_l, 1)

            b0 = Num(0, 0)
            stats(b0, b0 + 1, 0)
            V.memset(val[:, :, :, :, :], 0.0).then_inc(s_const_dve, 1)
            V.memset(ev[:, :, :], 0.0).then_inc(s_const_dve, 1)
            V.memset(bias[:, 0, :, WIN:S], 0.0)
            V.memset(bias[:, 1, :, 0:R], 0.0).then_inc(s_const_dve, 1)
            dve.wait_ge(s_const_dve, 3)
            V.memset(val[:, :, :, :, HD:HD + 1], 1.0)
            dve.wait_ge(s_const, 16 * 12)
            V.tensor_copy(sel[:, :, :].rearrange("p g m -> p (g m)"), sel_f)
            V.tensor_copy(pick[:, :, :].rearrange("p e m -> p (e m)"), pick_f)
            for c in range(NC):
                V.tensor_scalar(ek_w[:, c, :], ek_w[:, c, :], ek_r[:, c:c + 1], None,
                                ALU.subtract).then_inc(s_const_dve, 1)
            dve.wait_ge(s_const_dve, 5)
            V.tensor_copy(ek_hi[:, :, :], ek_w[:, :, :]).then_inc(s_const_dve, 1)
            dve.wait_ge(s_const_dve, 6)
            V.tensor_tensor(ek_w[:, :, :], ek_w[:, :, :], ek_hi[:, :, :].bitcast(F32),
                            ALU.subtract).then_inc(s_const_dve, 1)
            V.tensor_scalar(ek_hi[:, :, :], ek_hi[:, :, :].bitcast(F32), mask[:, 0:1], None,
                            ALU.mult).then_inc(s_const_dve, 1)
            dve.wait_ge(s_const_dve, 8)
            V.scalar_tensor_tensor(ek[:, :, :], ek_w[:, :, :], mask[:, 1:2], ek_hi[:, :, :].bitcast(F32),
                                   ALU.mult, ALU.add)
            for c in range(NC):
                V.tensor_tensor(ev[:, c, 0:HD], ev_r[:, :], edge[:, 1 - c, 0:HD], ALU.subtract)
                V.tensor_tensor(ev_tail[:, c, :], edge[:, c, :], edge[:, 1 - c, :],
                                ALU.subtract).then_inc(s_const_dve, 1)
            V.memset(t2[:, :], 0.0).then_inc(s_boot, 1)
            take_qk(b0)
            lo_parts(b0)
            take_values(b0, 0)
            for n in range(UH):
                take_l(b0, n)

            def body(t):
                for s in range(4):
                    u = t * 4 + s
                    for n in range(UH):
                        q = s * UH + n
                        k = t - 2
                        for kk, ee in ([(k, q // 4 + 1)] if q % 4 == 2 and q < 28 else [(k + 1, 0)] if q == 30 else []):
                            if 0 <= kk.i < NK:
                                x_e = kk * NE + ee
                                dve.wait_ge(s_wb_ps, (x_e + 1).v)
                                if x_e.i >= 2:
                                    dve.wait_ge(s_h1, ((x_e - 1) * NM).v)
                                V.tensor_tensor(xg[:, ee % 2, :], xs[:, :] if ee == 0 else xw[:, :], RT[:, :],
                                                ALU.mult).then_inc(s_xg, 1)
                        if u.i < NU:
                            ready0 = counted(dve, counts[0], u * UH + n + 1)
                            if n % 4 == 0:
                                ready1 = counted(dve, counts[1], u * 32 + 32)
                            if u.i > 0 or n > 1:
                                ready2 = counted(dve, counts[2], u * 16 + 2 * n - 2)
                            dve.wait_ge(s_const, 16 * 12)
                            dve.wait_ge(s_s, ready0)
                            if n % 4 == 0:
                                dve.wait_ge(s_br[n // 4], ready1)
                            if u.i > 0 or n > 1:
                                dve.wait_ge(s_exp, ready2)
                            for c in range(NC):
                                V.tensor_tensor_reduce(out=sneg[:, n % 2, c, :], in0=SB_[:, S * c:S * c + S],
                                                       in1=bias[:, c, n, :], scale=-1.0, scalar=BIG,
                                                       op0=ALU.add, op1=ALU.min,
                                                       accum_out=nmax[:, n % 2, c:c + 1]).then_inc(s_ttr, 1)
                        if u.i + 1 < NU:
                            take_l(u + 1, n)
                        if q % 2 == 1 and 0 <= k.i < NK:
                            p = q // 2
                            kp = k * 16 + p
                            dve.wait_ge(s_th, (kp + 1).v)
                            V.scalar_tensor_tensor(th[:, :], th[:, :], 1.0, H0[:, :], ALU.add,
                                                   ALU.mult).then_inc(s_ag, 1)
                            dve.wait_ge(s_ag, (kp + 1).v)
                            dve.wait_ge(s_h1, (kp + 1).v)
                            if kp.i >= 2:
                                dve.wait_ge(s_wo, (kp - 1).v)
                            V.tensor_tensor(ug[:, p % 2, :], th[:, :], H1[:, :], ALU.mult).then_inc(s_ug, 1)
                        v = u - 1
                        if 0 <= v.i < NU and n in (1, 5):
                            hf = n // 4
                            dve.wait_ge(s_pr[hf], (v * 32 + 32).v)
                            bp = ((s - 1) // 2) % 2
                            h0 = UH * ((s + 1) % 2) + HU * hf
                            if v.i >= 4 and n == 1 and s % 2 == 1:
                                dve.wait_ge(s_t1, ((t * 2 + (s - 1) // 2) * 2 - 2).v)
                            for c, at in ((0, 0), (1, P)):
                                V.tensor_reduce(tail[:, bp, c, h0:h0 + HU], prel[:, c, HU * hf:HU * hf + HU, at:at + R],
                                                AX.X, ALU.add).then_inc(s_tail, 1)
                        if s % 2 == 0:
                            b = t * 2 + s // 2 + 1
                            par = (s // 2 + 1) % 2
                            if b.i < NB:
                                if n == 0:
                                    stats(b, t + (1 if par == 1 else 2), par)
                                if n == 3:
                                    take_qk(b)
                                if n == 4:
                                    lo_parts(b)
                                if n == 6:
                                    take_stack(b, par, 1)
                            pb = t * 2 + s // 2 - 2
                            if 0 <= pb.i < NB:
                                if n == 0:
                                    dve.wait_ge(s_op_ps, (pb + 1).v)
                                    dve.wait_ge(s_xb, (pb + 1).v)
                                    if pb.i >= 1:
                                        dve.wait_ge(s_x1w, (pb * 16).v)
                                        dve.wait_ge(s_xn2, (pb * 2).v)
                                    V.tensor_tensor(x1[:, :, :], LX[:, 0:2 * D].rearrange("p (c d) -> p c d", c=NC),
                                                    xb[:, :, :], ALU.add).then_inc(s_x1, 1)
                                    dve.wait_ge(s_x1, (pb + 1).v)
                                    for c in range(NC):
                                        V.bn_stats(stat2[:, c, :], x1[:, c, :]).then_inc(s_st2, 1)
                                    for c in range(NC):
                                        ready = counted(dve, counts[0], pb * 2 + c + 1)
                                        dve.wait_ge(s_const, 16 * 12)
                                        dve.wait_ge(s_st2, ready)
                                        V.bn_aggr(mv2[:, c, :], stat2[:, c, :]).then_inc(s_mv2, 1)
                                if n == 4:
                                    dve.wait_ge(s_g_ps, (pb + 1).v)
                                    V.tensor_copy(lg[:, :, :], LX[:, 0:2 * NE].rearrange("p (c e) -> p c e", c=NC)) \
                                        .then_inc(s_lg, 1)
                                    ready = counted(dve, counts[0], pb + 1)
                                    dve.wait_ge(s_const, 16 * 12)
                                    dve.wait_ge(s_lg, ready)
                                    for c in range(NC):
                                        V.max(top[:, c, :], lg[:, c, :]).then_inc(s_top, 1)
                                    for c in range(NC):
                                        ready = counted(dve, counts[0], pb * 2 + c + 1)
                                        dve.wait_ge(s_const, 16 * 12)
                                        dve.wait_ge(s_top, ready)
                                        V.max_index(topi[:, c, :], top[:, c, :], lg[:, c, :]).then_inc(s_topi, 1)
                                    V.tensor_tensor(gd[:, :], top[:, :, 1], top[:, :, 0],
                                                    ALU.subtract).then_inc(s_gd, 1)
                                    dve.wait_ge(s_topi, (pb * 2 + 2).v)
                                    V.tensor_copy(topf[:, :, :], topi[:, :, :]).then_inc(s_topf, 1)
                                if n == 6:
                                    dve.wait_ge(s_ge, (pb + 1).v)
                                    V.tensor_scalar(gs[:, :], ge[:, :], 2.0, 2.0, ALU.mult, ALU.add).then_inc(s_gs, 1)
                                    dve.wait_ge(s_gs, (pb + 1).v)
                                    V.reciprocal(gp[:, 0, :], gs[:, :]).then_inc(s_gp1, 1)
                                    dve.wait_ge(s_gp1, (pb + 1).v)
                                    V.tensor_tensor(gp[:, 1, :], ge[:, :], gp[:, 0, :], ALU.mult).then_inc(s_gp2, 1)
                                    dve.wait_ge(s_topf, (pb + 1).v)
                                    dve.wait_ge(s_gp2, (pb + 1).v)
                                    for c in range(NC):
                                        for i, w_ in ((0, wa), (1, wb)):
                                            V.tensor_scalar(w_[:, c, :], iota[:, :], topf[:, c, i:i + 1],
                                                            gp[:, i, c:c + 1], ALU.is_equal, ALU.mult).then_inc(s_oh, 1)
                                    dve.wait_ge(s_oh, (pb * 4 + 4).v)
                                    V.tensor_tensor(wf[:, :, :], wa[:, :, :], wb[:, :, :], ALU.add).then_inc(s_wf, 1)
                                    dve.wait_ge(s_wf, (pb + 1).v)
                                    if pb.i >= 1:
                                        dve.wait_ge(s_ws_ps, (pb * 1).v)
                                    V.tensor_copy(wr[:, :, 0:NE], wf[:, :, :]).then_inc(s_wh, 1)
                                    dve.wait_ge(s_wh, (pb + 1).v)
                                    V.tensor_tensor(wr[:, :, NE:2 * NE], wf[:, :, :], wr[:, :, 0:NE].bitcast(F32),
                                                    ALU.subtract).then_inc(s_wl, 1)
                        else:
                            b = t * 2 + (s - 1) // 2 + 1
                            par = ((s - 1) // 2 + 1) % 2
                            if b.i < NB:
                                if n == 1:
                                    take_stack(b, par, 3)
                                if n == 2:
                                    take_values(b, par)
                            pb = t * 2 + (s - 3) // 2
                            if 0 <= pb.i < NB and n in (3, 4):
                                c = n - 3
                                i = pb * 2 + c
                                rows = LX[:, :].rearrange("p (h v) -> p h v", v=VS)
                                dve.wait_ge(s_cx_ps, (i + 1).v)
                                dve.wait_ge(s_t1, (i + 1).v)
                                if i.i > 0:
                                    dve.wait_ge(s_t3, (i * 1).v)
                                V.reciprocal(rz[:, :], rows[:, :, HD]).then_inc(s_rz, 1)
                                V.tensor_tensor(t2[:, :].rearrange("p (h d) -> p h d", d=HD), rows[:, :, 0:HD],
                                                t1[:, c, :].rearrange("p (h d) -> p h d", d=HD), ALU.add).then_inc(s_t2, 1)
                                dve.wait_ge(s_rz, (i + 1).v)
                                dve.wait_ge(s_t2, (i + 1).v)
                                if pb.i >= 1:
                                    dve.wait_ge(s_cn, (i - 1).v)
                                V.tensor_tensor(t3[:, c, :].rearrange("p (h d) -> p h d", d=HD),
                                                t2[:, :].rearrange("p (h d) -> p h d", d=HD),
                                                rz[:, :].unsqueeze(2).to_broadcast([P, H, HD]), ALU.mult).then_inc(s_t3, 1)
                        kf = t - 3
                        if s == 1 and n == 5 and 0 <= kf.i < NK:
                            dve.wait_ge(s_f_ps, (kf + 1).v)
                            dve.wait_ge(s_xo, (kf * 16 + 16).v)
                            V.tensor_tensor(xo[:, :, :], LX[:, :].rearrange("p (j d) -> p j d", d=D), xo[:, :, :],
                                            ALU.add).then_inc(s_fin, 1)

            iterations(dve, body)


def kernel(L0_attn_x, L0_attn_W_qkv, L0_attn_b_qkv, L0_attn_W_out, L0_attn_b_out, L0_attn_rel_emb_k,
           L0_attn_rel_emb_v, L0_ffn_gate_kernel, L0_ffn_w0_kernel, L0_ffn_w1_kernel, L0_ffn_wo_kernel):
    import concourse.bacc as bacc
    from concourse.bass_utils import run_bass_kernel_spmd

    def c_(a):
        return np.ascontiguousarray(a)

    b_qkv = np.asarray(L0_attn_b_qkv)
    rk, rv = np.asarray(L0_attn_rel_emb_k), np.asarray(L0_attn_rel_emb_v)
    w = np.arange(WIN)
    offs = (np.clip(w - R + 1, 0, 2 * R), np.minimum(w + 1, 2 * R))
    refs = (2 * R, 0)
    d_of = np.arange(P) % HD
    ek_win = c_(np.stack([rk[o][:, d_of].T for o in offs], axis=1))
    ek_ref = c_(np.stack([rk[r][d_of] for r in refs], axis=1))
    ev_edge = c_(np.stack([np.broadcast_to(np.tile(rv[r], H), (P, D)) for r in (0, 2 * R)], axis=1))
    sel = np.zeros((P, 16, P), np.float32)
    for g in range(4):
        for kind, parts in enumerate(((0, 1), (2, 3), (0, 2), (1, 3))):
            for j in range(4):
                for s in parts:
                    for d in range(HD):
                        sel[HD * (4 * g + j) + d, 4 * g + kind, 32 * j + HD * s + d] = 1.0
    pick = np.zeros((2 * NE, NE, P), np.float32)
    for e in range(NE):
        pick[e, e], pick[NE + e, e] = 1.0, 1.0
    part = (np.arange(P) % 32) // HD
    mask = c_(np.stack([part % 2 == 0, part % 2 == 1], axis=1).astype(np.float32))
    arrays = {
        "x": c_(np.asarray(L0_attn_x).reshape(NB * S, D)), "w_qkv": c_(L0_attn_W_qkv), "w_out": c_(L0_attn_W_out),
        "gate": c_(L0_ffn_gate_kernel), "w0": c_(L0_ffn_w0_kernel), "w1": c_(L0_ffn_w1_kernel),
        "wo": c_(L0_ffn_wo_kernel), "bqk": c_(b_qkv[:2 * D].reshape(2, D).T),
        "bv": c_(np.broadcast_to(b_qkv[2 * D:], (P, D))), "bout": c_(np.broadcast_to(np.asarray(L0_attn_b_out), (P, D))),
        "ek_win": ek_win, "ek_ref": ek_ref, "ev_rows": c_(rv[1:]), "ev_edge": ev_edge,
        "ident_in": np.eye(P, dtype=np.float32), "sel_in": sel, "pick_in": pick,
        "iota_in": c_(np.broadcast_to(np.arange(NE, dtype=np.float32), (P, NE))), "mask_in": mask,
    }
    nc = bacc.Bacc("TRN2", target_bir_lowering=False, num_devices=1)
    aps = [nc.dram_tensor(n, a.shape, mybir.dt.from_np(a.dtype), kind="ExternalInput").ap() for n, a in arrays.items()]
    out = nc.dram_tensor("out", (NB * S, D), F32, kind="ExternalOutput").ap()
    layer_program(nc, *aps, out)
    r = run_bass_kernel_spmd(nc, [arrays], core_ids=[0])
    return r.results[0]["out"].reshape(NB, S, D)
```

```python
from contextlib import ExitStack

import numpy as np

import concourse.bass as bass
from concourse import mybir
from concourse.alu_op_type import AluOpType as ALU

F32 = mybir.dt.float32
F32R = mybir.dt.float32r
U32 = mybir.dt.uint32
ACT = mybir.ActivationFunctionType
AX = mybir.AxisListType

P = 128
NB, S, D = 32, 256, 128
H, HD = 16, 8
R = 64
NC = S // P
UH = 8
HU = 4
NU = NB * H // UH
NE, HID = 8, 256
NM = HID // P
BT = 512
NK = NB * S // BT
WIN = R + P
PITCH = WIN + P
VS = 32
EPS = 1e-5
BIG = 3.0e38


def counted(eng, reg, count):
    if isinstance(count.v, int):
        return count.v
    eng.reg_mov(reg, count.v)
    return reg


class Num:

    def __init__(self, v, i):
        self.v, self.i = v, i

    def __mul__(self, k):
        return Num(self.v * k, self.i * k)

    def __add__(self, k):
        return Num(self.v + k, self.i + k)

    def __sub__(self, k):
        return self + (-k)


def layer_program(nc, x, w_qkv, w_out, gate, w0, w1, wo, bqk, bv, bout, ek_win, ek_ref, ev_rows, ev_edge,
                  ident_in, sel_in, pick_in, iota_in, mask_in, out):
    ctx = ExitStack()
    with ctx:
        def sb(name, shape, dt=F32):
            return ctx.enter_context(nc.sbuf_tensor(name, shape, dt))

        def bank(name):
            return ctx.enter_context(nc.psum_tensor(name, [P, 512], F32))

        def sem(name):
            return ctx.enter_context(nc.semaphore(name))

        ident = sb("ident", [P, P])
        sel = sb("sel", [P, 16, P], F32R)
        pick = sb("pick", [16, NE, P], F32R)
        iota = sb("iota", [P, NE])
        mask = sb("mask", [P, 2])
        wqkv_sb = sb("wqkv_sb", [P, 3 * D])
        wout_sb = sb("wout_sb", [P, D])
        gate_sb = sb("gate_sb", [P, NE])
        w01_hi = sb("w01_hi", [P, 2, NE, HID], F32R)
        w01_lo = sb("w01_lo", [P, 2, NE, HID], F32R)
        wo_sb = sb("wo_sb", [P, NE, NM, D])
        bqk_sb = sb("bqk_sb", [P, 2])
        bv_sb = sb("bv_sb", [P, D])
        bout_sb = sb("bout_sb", [P, D])
        ek_r = sb("ek_r", [P, NC])
        ek = sb("ek", [P, NC, WIN], F32R)
        ev_r = sb("ev_r", [P, HD])
        edge = sb("edge", [P, 2, D])
        ev = sb("ev", [P, NC, VS])
        ev_tail = sb("ev_tail", [P, NC, D])

        xt = sb("xt", [P, 2, NC, D])
        stat = sb("stat", [P, NC, 6])
        mv = sb("mv", [P, NC, 2])
        mhalf = sb("mhalf", [P, NC])
        vare = sb("vare", [P, NC])
        rstd = sb("rstd", [P, NC])
        xn = sb("xn", [P, NC, D])
        xnT = sb("xnT", [P, S])
        cnT = xnT
        qk32 = sb("qk32", [P, 2, S])
        qk_hi = sb("qk_hi", [P, 2, S], F32R)
        qk_lo = sb("qk_lo", [P, 2, S], F32R)
        qk = sb("qk", [P, 2, 4, 2, S], F32R)
        val = sb("val", [P, 2, NC, H, VS])
        lrow = sb("lrow", [P, 2, NC, HU, WIN])
        bias = sb("bias", [P, NC, UH, S])
        sneg = sb("sneg", [P, 2, NC, S])
        nmax = sb("nmax", [P, 2, NC])
        prob = sb("prob", [P, 2, NC, UH, S])
        prel = sb("prel", [P, NC, UH, WIN])
        tail = sb("tail", [P, 2, NC, H])
        pT = sb("pT", [P, 2, NC, S])
        rT = sb("rT", [P, 2, S])
        cT = sb("cT", [P, 4, S])
        t1 = sb("t1", [P, NC, D])
        rz = sb("rz", [P, H])
        cn = sb("cn", [P, NC, D])
        t2 = t3 = cn
        xb = sb("xb", [P, NC, D])
        x1 = sb("x1", [P, NC, D])

        stat2 = sb("stat2", [P, NC, 6])
        mv2 = sb("mv2", [P, NC, 2])
        vare2 = sb("vare2", [P, NC])
        rstd2 = sb("rstd2", [P, NC])
        xn2 = sb("xn2", [P, NC, D])
        lg = sb("lg", [P, NC, NE])
        top = sb("top", [P, NC, 8])
        topi = sb("topi", [P, NC, 8], U32)
        topf = sb("topf", [P, NC, 8])
        gd = sb("gd", [P, NC])
        ge = sb("ge", [P, NC])
        gs = sb("gs", [P, NC])
        gp = sb("gp", [P, 2, NC])
        wa = sb("wa", [P, NC, NE])
        wb = sb("wb", [P, NC, NE])
        wf = sb("wf", [P, NC, NE])
        wr = sb("wr", [P, NC, 2 * NE], F32R)

        xs = sb("xs", [P, BT])
        xw_hi = sb("xw_hi", [P, BT], F32R)
        xw_lo = sb("xw_lo", [P, BT], F32R)
        ws = sb("ws", [2 * NE, BT], F32R)
        ww = sb("ww", [2 * NE, BT], F32R)
        we = sb("we", [P, 2, BT])
        ffn = sb("ffn", [P, 4, BT])
        th, ug, oT = ffn[:, 0, :], ffn[:, 1, :], ffn[:, 2, :]
        xo = ffn[:, 3, :].rearrange("p (j d) -> p j d", j=4)
        stage = ffn[:, :, :].rearrange("p j t -> p (j t)")

        boot = prob[:, 0, :, :, :].rearrange("p c h k -> p (c h k)")
        sel_f = boot[:, 0:16 * P]
        pick_f = boot[0:2 * NE, 16 * P:(16 + NE) * P]
        ek_hi = stage[:, 3 * BT:3 * BT + NC * WIN].rearrange("p (c w) -> p c w", c=NC).bitcast(F32R)
        ek_w = boot[:, (16 + NE) * P:(16 + NE) * P + NC * WIN].rearrange("p (c w) -> p c w", c=NC)

        SB_, LX, PT, RT, PV, H0, H1, OB = (bank(n) for n in ("s_b", "lx_b", "pt_b", "rt_b", "pv_b", "h0_b", "h1_b", "o_b"))

        lscr = nc.dram_tensor("lscr", [2, NC, P, HU, PITCH], F32, kind="Internal").ap()
        pscr = nc.dram_tensor("pscr", [2, NC, P, HU, PITCH], F32, kind="Internal").ap()
        x1d = nc.dram_tensor("x1d", [NB * S, D], F32, kind="Internal").ap()
        CST, IST = P * HU * PITCH, HU * PITCH

        def by_key(half, c):
            return bass.AP(lscr.tensor, (half * NC + c) * CST + P - 1, [[IST - 1, P], [PITCH, HU], [1, WIN]])

        def by_offset(half, c):
            return bass.AP(pscr.tensor, (half * NC + c) * CST + c, [[IST + 1, P], [PITCH, HU], [1, WIN]])

        x_v = x.rearrange("(b c p) d -> b p c d", c=NC, p=P)
        x1_v = x1d.rearrange("(b c p) d -> b p c d", c=NC, p=P)
        x1_kv = x1d.rearrange("(k j p) d -> k p j d", j=4, p=P)
        out_v = out.rearrange("(k j p) d -> k p j d", j=4, p=P)

        s_const, s_const2 = sem("s_const"), sem("s_const2")
        s_zero, s_margin = sem("s_zero"), sem("s_margin")
        s_const_dve, s_boot = sem("s_const_dve"), sem("s_boot")
        s_x = [sem(f"s_xin{i}") for i in range(2)]
        s_mh, s_ve, s_ve2 = sem("s_mh"), sem("s_ve"), sem("s_ve2")
        s_st, s_mv, s_rs = sem("s_st"), sem("s_mv"), sem("s_rs")
        s_xn = sem("s_xn")
        s_xnT_ps, s_xnT = sem("s_xnT_ps"), sem("s_xnT")
        s_qk_ps, s_qk32 = sem("s_qk_ps"), sem("s_qk32")
        s_hi, s_lo = sem("s_hi"), sem("s_lo")
        s_stk_ps, s_stk = sem("s_stk_ps"), sem("s_stk")
        s_v_ps, s_v = sem("s_v_ps"), sem("s_v")
        s_l_ps, s_l = sem("s_l_ps"), sem("s_l")
        s_lw = [sem(f"s_lw{i}") for i in range(2)]
        s_br = [sem(f"s_br{i}") for i in range(2)]
        s_s, s_ttr = sem("s_s"), sem("s_ttr")
        s_exp = sem("s_exp")
        s_pw = [sem(f"s_pw{i}") for i in range(2)]
        s_pr = [sem(f"s_pr{i}") for i in range(2)]
        s_tail = sem("s_tail")
        s_pt_ps, s_pt = sem("s_pt_ps"), sem("s_pt")
        s_rt_ps, s_rt = sem("s_rt_ps"), sem("s_rt")
        s_pv, s_cT = sem("s_pv"), sem("s_cT")
        s_cx_ps = sem("s_cx_ps")
        s_t1, s_rz, s_t2, s_t3, s_cn = (sem(n) for n in ("s_t1", "s_rz", "s_t2", "s_t3", "s_cn"))
        s_cnT_ps, s_cnT = sem("s_cnT_ps"), sem("s_cnT")
        s_xr, s_xb = sem("s_xr"), sem("s_xb")
        s_op_ps, s_x1, s_x1w = sem("s_op_ps"), sem("s_x1"), sem("s_x1w")
        s_st2, s_mv2, s_rs2, s_xn2 = sem("s_st2"), sem("s_mv2"), sem("s_rs2"), sem("s_xn2")
        s_xs_ps, s_xs = sem("s_xs_ps"), sem("s_xs")
        s_g_ps, s_lg = sem("s_g_ps"), sem("s_lg")
        s_top, s_topi, s_topf, s_gd, s_ge = sem("s_top"), sem("s_topi"), sem("s_topf"), sem("s_gd"), sem("s_ge")
        s_gs, s_gp1, s_gp2, s_oh, s_wf, s_wh, s_wl = (sem(n) for n in ("s_gs", "s_gp1", "s_gp2", "s_oh", "s_wf", "s_wh", "s_wl"))
        s_ws_ps, s_ws = sem("s_ws_ps"), sem("s_ws")
        s_ww = sem("s_ww")
        s_xw_hi, s_xw_lo = sem("s_xw_hi"), sem("s_xw_lo")
        s_wb_ps, s_we = sem("s_wb_ps"), sem("s_we")
        s_stage, s_part = sem("s_stage"), sem("s_part")
        s_h0, s_h1, s_th, s_ag, s_agw, s_ug, s_wo = (sem(n) for n in ("s_h0", "s_h1", "s_th", "s_ag", "s_agw",
                                                                      "s_ug", "s_wo"))
        s_oT, s_f_ps, s_fin, s_xo, s_out = sem("s_oT"), sem("s_f_ps"), sem("s_fin"), sem("s_xo"), sem("s_out")

        LOOP = (4, 15)
        LAST = NK + 2

        def iterations(eng, body):
            for i in range(LOOP[0]):
                body(Num(i, i))
            with eng.Fori(*LOOP) as t:
                body(Num(t, LOOP[0] + 1))
            for i in range(LOOP[1], LAST + 1):
                body(Num(i, i))

        block = ctx.enter_context(nc.Block())

        @block.sync
        def _(sp):
            counts = [sp.alloc_register(f"sp_count{i}") for i in range(3)]
            sp.dma_start(xt[:, 0, :, :], x_v[0]).then_inc(s_x[0], 16)
            sp.dma_start(xt[:, 1, :, :], x_v[1]).then_inc(s_x[1], 16)
            for dst, src in ((ident[:, :], ident_in), (iota[:, :], iota_in), (mask[:, :], mask_in),
                             (wqkv_sb[:, :], w_qkv), (bqk_sb[:, :], bqk), (bv_sb[:, :], bv),
                             (sel_f, sel_in.rearrange("p g m -> p (g m)")), (ek_w, ek_win), (ek_r[:, :], ek_ref), (ev_r[:, :], ev_rows),
                             (edge[:, :, :], ev_edge), (pick_f, pick_in.rearrange("p e m -> p (e m)"))):
                sp.dma_start(dst, src).then_inc(s_const, 16)
            sp.wait_ge(s_zero, 1)
            zv = sneg[:, 0, :, :].rearrange("p c (h m) -> p (c h) m", h=2)
            for half in range(2):
                for scr, (m0, m1) in ((lscr, (WIN, 0)), (pscr, (0, WIN))):
                    sp.dma_start(scr[half, 0, :, :, m0:m0 + P], zv).then_inc(s_margin, 16)
                    sp.dma_start(scr[half, 1, :, :, m1:m1 + P], zv).then_inc(s_margin, 16)
            for dst, src in ((wout_sb[:, :], w_out), (bout_sb[:, :], bout), (gate_sb[:, :], gate),
                             (wo_sb[:, :, :, :], wo.rearrange("n (m p) e -> p n m e", p=P))):
                sp.dma_start(dst, src).then_inc(s_const2, 16)
            sp.wait_ge(s_margin, 16 * 8)

            def store_l(u, half):
                ready0 = counted(sp, counts[0], u * UH + HU * (half + 1))
                if u.i >= 1:
                    ready1 = counted(sp, counts[1], u * 32)
                sp.wait_ge(s_margin, 16 * 8)
                sp.wait_ge(s_l, ready0)
                if u.i >= 1:
                    sp.wait_ge(s_br[half], ready1)
                for c, at in ((0, 0), (1, P)):
                    sp.dma_start(lscr[half, c, :, :, at:at + WIN], lrow[:, half, c, :, :]).then_inc(s_lw[half], 16)

            def load_bias(u, half):
                ready0 = counted(sp, counts[0], u * 32 + 32)
                if u.i >= 1:
                    ready1 = counted(sp, counts[1], (u - 1) * 16 + 8 * (half + 1))
                sp.wait_ge(s_margin, 16 * 8)
                sp.wait_ge(s_lw[half], ready0)
                if u.i >= 1:
                    sp.wait_ge(s_ttr, ready1)
                heads = slice(HU * half, HU * half + HU)
                for c in range(NC):
                    sp.dma_start(bias[:, c, heads, R * c:R * c + WIN], by_key(half, c)).then_inc(s_br[half], 16)

            def store_p(u, half, par):
                ready0 = counted(sp, counts[0], u * 16 + 8 * (half + 1))
                if u.i >= 1:
                    ready1 = counted(sp, counts[1], u * 32)
                sp.wait_ge(s_margin, 16 * 8)
                sp.wait_ge(s_exp, ready0)
                if u.i >= 1:
                    sp.wait_ge(s_pr[half], ready1)
                heads = slice(HU * half, HU * half + HU)
                for c, at in ((0, P - 1), (1, 0)):
                    sp.dma_start(pscr[half, c, :, :, at:at + WIN],
                                 prob[:, par, c, heads, R * c:R * c + WIN]).then_inc(s_pw[half], 16)

            def load_prel(u, half):
                ready0 = counted(sp, counts[0], u * 32 + 32)
                if u.i >= 1:
                    ready1 = counted(sp, counts[1], (u - 1) * UH + HU * (half + 1))
                    ready2 = counted(sp, counts[2], (u - 1) * 4 + 2 * (half + 1))
                sp.wait_ge(s_margin, 16 * 8)
                sp.wait_ge(s_pw[half], ready0)
                if u.i >= 1:
                    sp.wait_ge(s_rt_ps, ready1)
                    sp.wait_ge(s_tail, ready2)
                heads = slice(HU * half, HU * half + HU)
                for c in range(NC):
                    sp.dma_start(prel[:, c, heads, :], by_offset(half, c)).then_inc(s_pr[half], 16)

            for half in range(2):
                store_l(Num(0, 0), half)
                load_bias(Num(0, 0), half)

            def body(t):
                for s in range(4):
                    u = t * 4 + s
                    for n in range(UH):
                        if n in (0, 4):
                            half = 1 if n == 0 else 0
                            pu, lu = (u - 1, u) if n == 0 else (u, u + 1)
                            if 0 <= pu.i < NU:
                                store_p(pu, half, (s + 1) % 2 if n == 0 else s % 2)
                            if 1 <= lu.i < NU:
                                store_l(lu, half)
                            if 0 <= pu.i < NU:
                                load_prel(pu, half)
                            if 1 <= lu.i < NU:
                                load_bias(lu, half)
                        if t.i == 0 and s < 2 and n == 1:
                            if s == 0:
                                sp.wait_ge(s_boot, 1)
                            else:
                                sp.wait_ge(s_part, 2)
                            sp.dma_start(stage.rearrange("p (n h) -> p n h", n=NE),
                                         (w0, w1)[s].rearrange("n e h -> e n h")).then_inc(s_stage, 16)
                        if s % 2 == 0:
                            b = t * 2 + s // 2
                            if n == 3 and b.i + 2 < NB:
                                ready = counted(sp, counts[0], b * 2 + 2)
                                sp.wait_ge(s_margin, 16 * 8)
                                sp.wait_ge(s_xn, ready)
                                sp.dma_start(xt[:, (s // 2) % 2, :, :], x_v[(b + 2).v]).then_inc(s_x[(s // 2) % 2], 16)
                            if n == 2 and 0 <= b.i - 2 < NB:
                                pb = b - 2
                                ready = counted(sp, counts[0], pb + 1)
                                sp.wait_ge(s_margin, 16 * 8)
                                sp.wait_ge(s_x1, ready)
                                sp.dma_start(x1_v[pb.v], x1[:, :, :]).then_inc(s_x1w, 16)
                        else:
                            b = t * 2 + (s - 3) // 2
                            if n == 2 and 0 <= b.i < NB:
                                if b.i >= 1:
                                    ready = counted(sp, counts[0], b * 1)
                                sp.wait_ge(s_margin, 16 * 8)
                                if b.i >= 1:
                                    sp.wait_ge(s_x1, ready)
                                sp.dma_start(xb[:, :, :], x_v[b.v]).then_inc(s_xr, 16)
                        k = t - 3
                        if s in (1, 2) and 0 <= k.i < NK:
                            if s == 1 and n == 1:
                                ready0 = counted(sp, counts[0], k * 32 + 32)
                                if k.i >= 1:
                                    ready1 = counted(sp, counts[1], k * 16)
                                sp.wait_ge(s_margin, 16 * 8)
                                sp.wait_ge(s_x1w, ready0)
                                if k.i >= 1:
                                    sp.wait_ge(s_out, ready1)
                                sp.dma_start(xo[:, :, :], x1_kv[k.v]).then_inc(s_xo, 16)
                            if s == 2 and n == 0:
                                ready = counted(sp, counts[0], k + 1)
                                sp.wait_ge(s_margin, 16 * 8)
                                sp.wait_ge(s_fin, ready)
                                sp.dma_start(out_v[k.v], xo[:, :, :]).then_inc(s_out, 16)

            iterations(sp, body)
            sp.wait_ge(s_x1w, 16 * NB)
            sp.wait_ge(s_out, 16 * NK)

        @block.gpsimd
        def _(gp_):
            counts = [gp_.alloc_register(f"gp__count{i}") for i in range(3)]
            gp_.memset(sneg[:, 0, :, :], 0.0).then_inc(s_zero, 1)

            def rstd_1(b):
                if b.i >= 1:
                    ready0 = counted(gp_, counts[0], b * 2)
                ready1 = counted(gp_, counts[1], b * 2 + 2)
                gp_.wait_ge(s_zero, 1)
                if b.i >= 1:
                    gp_.wait_ge(s_xn, ready0)
                gp_.wait_ge(s_mv, ready1)
                gp_.tensor_scalar(vare[:, :], mv[:, :, 1], EPS, None, ALU.add).then_inc(s_ve, 1)
                gp_.wait_ge(s_ve, (b + 1).v)
                gp_.tensor_tensor(rstd[:, :], vare[:, :], mhalf[:, :], ALU.pow).then_inc(s_rs, 1)

            gp_.memset(mhalf[:, :], -0.5).then_inc(s_mh, 1)
            gp_.wait_ge(s_mh, 1)
            rstd_1(Num(0, 0))
            rstd_1(Num(1, 1))
            gp_.wait_ge(s_boot, 1)

            def body(t):
                for s in range(4):
                    for n in range(UH):
                        q = s * UH + n
                        if s % 2 == 0:
                            pb = t * 2 + s // 2 - 2
                            if n == 2 and 0 <= pb.i < NB:
                                if pb.i >= 1:
                                    ready0 = counted(gp_, counts[0], pb * 2)
                                ready1 = counted(gp_, counts[1], pb * 2 + 2)
                                gp_.wait_ge(s_zero, 1)
                                if pb.i >= 1:
                                    gp_.wait_ge(s_xn2, ready0)
                                gp_.wait_ge(s_mv2, ready1)
                                gp_.tensor_scalar(vare2[:, :], mv2[:, :, 1], EPS, None, ALU.add).then_inc(s_ve2, 1)
                                gp_.wait_ge(s_ve2, (pb + 1).v)
                                gp_.tensor_tensor(rstd2[:, :], vare2[:, :], mhalf[:, :], ALU.pow).then_inc(s_rs2, 1)
                        else:
                            nb = t * 2 + s // 2 + 2
                            if n == 7 and nb.i < NB:
                                rstd_1(nb)
                            pb = t * 2 + (s - 3) // 2
                            par = ((s - 3) // 2) % 2
                            if 0 <= pb.i < NB:
                                if n == 2:
                                    gp_.wait_ge(s_tail, (pb * 8 + 8).v)
                                    if pb.i >= 1:
                                        gp_.wait_ge(s_t2, (pb * 2).v)
                                    for c in range(NC):
                                        gp_.tensor_tensor(t1[:, c, :].rearrange("p (h d) -> p h d", d=HD),
                                                          tail[:, par, c, :].unsqueeze(2).to_broadcast([P, H, HD]),
                                                          ev_tail[:, c, :].rearrange("p (h d) -> p h d", d=HD),
                                                          ALU.mult).then_inc(s_t1, 1)
                                if n in (4, 5):
                                    c = n - 4
                                    gp_.wait_ge(s_t3, (pb * 2 + c + 1).v)
                                    gp_.tensor_tensor(cn[:, c, :], t3[:, c, :], edge[:, 1 - c, :],
                                                      ALU.add).then_inc(s_cn, 1)
                                if n == 6:
                                    gp_.wait_ge(s_xr, (pb * 16 + 16).v)
                                    if pb.i == 0:
                                        gp_.wait_ge(s_const2, 16 * 4)
                                    gp_.tensor_tensor(xb[:, :, :], xb[:, :, :],
                                                      bout_sb[:, :].unsqueeze(1).to_broadcast([P, NC, D]),
                                                      ALU.add).then_inc(s_xb, 1)
                        if t.i == 0 and s < 2 and n == 4:
                            w_hi, w_lo = (w[:, s, :, :].rearrange("p n h -> p (n h)") for w in (w01_hi, w01_lo))
                            gp_.wait_ge(s_stage, 16 * (s + 1))
                            gp_.tensor_copy(w_hi, stage).then_inc(s_part, 1)
                            gp_.wait_ge(s_part, 2 * s + 1)
                            gp_.tensor_tensor(w_lo, stage, w_hi.bitcast(F32), ALU.subtract).then_inc(s_part, 1)
                        k = t - 2
                        if 0 <= k.i < NK and q % 2 == 1 and t.i < NK:
                            kp = k * (NE * NM) + q // 2
                            gp_.wait_ge(s_ag, (kp + 1).v)
                            gp_.wait_ge(s_we, (k * NE + (q // 4 + 1)).v)
                            gp_.tensor_tensor(th, th, we[:, (q // 4) % 2, :], ALU.mult).then_inc(s_agw, 1)

            iterations(gp_, body)

        @block.tensor
        def _(pe):
            mm, tr = nc.tensor.matmul, nc.tensor.transpose
            lx = [[]]

            def lx_free():
                for taken, count in lx[0]:
                    if count.i > 0:
                        pe.wait_ge(taken, count.v)

            def rows_T(b):
                lx_free()
                pe.wait_ge(s_xn, (b * 2 + 2).v)
                for c in range(NC):
                    last = tr(LX[:, P * c:P * c + P], xn[:, c, :], ident[:, :])
                last.then_inc(s_xnT_ps, 1)
                lx[0] = [(s_xnT, b + 1)]

            def project(b):
                lx_free()
                pe.wait_ge(s_xnT, (b + 1).v)
                for w in range(2):
                    last = mm(LX[:, S * w:S * w + S], wqkv_sb[:, D * w:D * w + D], xnT[:, :], start=True, stop=True)
                last.then_inc(s_qk_ps, 1)
                lx[0] = [(s_qk32, b * 2 + 2)]

            def stack(b, g):
                lx_free()
                pe.wait_ge(s_hi, (b + 1).v)
                pe.wait_ge(s_lo, (b + 1).v)
                for w in range(2):
                    mm(LX[:, S * w:S * w + S], sel[:, 4 * g + 2 * w, :], qk_hi[:, w, :], start=True, stop=False)
                    last = mm(LX[:, S * w:S * w + S], sel[:, 4 * g + 2 * w + 1, :], qk_lo[:, w, :],
                              start=False, stop=True)
                last.then_inc(s_stk_ps, 1)
                lx[0] = [(s_stk, b * 4 + g + 1)]

            def values(b):
                lx_free()
                for c in range(NC):
                    last = mm(LX[:, D * c:D * c + D], xnT[:, P * c:P * c + P], wqkv_sb[:, 2 * D:3 * D],
                              start=True, stop=True)
                last.then_inc(s_v_ps, 1)
                lx[0] = [(s_v, b + 1)]

            def rel_logits(u, par, half, n):
                g, j = 2 * half + n // 4, n % 4
                lx_free()
                if n % 4 == 0:
                    pe.wait_ge(s_stk, (u * 2 + n // 4 + 1).v)
                rows = slice(32 * j, 32 * j + 32)
                for c in range(NC):
                    last = mm(LX[:, WIN * c:WIN * c + WIN], qk[rows, par, g, 0, P * c:P * c + P], ek[rows, c, :],
                              start=True, stop=True)
                last.then_inc(s_l_ps, 1)
                lx[0] = [(s_l, u * UH + n + 1)]

            def scores(u, par, half, n):
                g, j = 2 * half + n // 4, n % 4
                if u.i > 0 or n > 0:
                    pe.wait_ge(s_ttr, (u * 16 + 2 * n).v)
                rows = slice(32 * j, 32 * j + 32)
                for c in range(NC):
                    last = mm(SB_[:, S * c:S * c + S], qk[rows, par, g, 0, P * c:P * c + P], qk[rows, par, g, 1, :],
                              start=True, stop=True)
                last.then_inc(s_s, 1)

            def transposes(u, upar, n):
                if n < 2:
                    pe.wait_ge(s_exp, (u * 16 + 14 + 2 * n).v)
                if u.i > 0 or n > 0:
                    pe.wait_ge(s_pt, (u * UH + n).v)
                for kc in range(NC):
                    for c in range(NC):
                        last = tr(PT[:, S * kc + P * c:S * kc + P * c + P], prob[:, upar, c, n, P * kc:P * kc + P],
                                  ident[:, :])
                last.then_inc(s_pt_ps, 1)

            def band_transposes(u, n, spread):
                if u.i > 0 or n > 0:
                    pe.wait_ge(s_rt, (u * UH + n).v)
                if spread is not None and spread.i > 0:
                    pe.wait_ge(s_we, spread.v)
                if n % 4 == 0:
                    pe.wait_ge(s_pr[n // 4], (u * 32 + 32).v)
                for c, at in ((0, R), (1, 0)):
                    last = tr(RT[:, P * c:P * c + P], prel[:, c, n, at:at + P], ident[:, :])
                last.then_inc(s_rt_ps, 1)

            def context(u, batches, par, half, n):
                if n == 0:
                    pe.wait_ge(s_v, batches.v)
                    if u.i > 0:
                        pe.wait_ge(s_cT, (u * 1).v)
                pe.wait_ge(s_pt, (u * UH + n + 2).v)
                pe.wait_ge(s_rt, (u * UH + n + 2).v)
                for kc in range(NC):
                    for m in (n, n + 1):
                        mm(o_of(m), val[:, par, kc, UH * half + m, :], pT[:, m % 2, kc, :], start=(kc == 0), stop=False)
                for c in range(NC):
                    for m in (n, n + 1):
                        last = mm(o_of(m)[:, P * c:P * c + P], ev[:, c, :], rT[:, m % 2, P * c:P * c + P],
                                  start=False, stop=(c == 1))
                        if c == 1:
                            last.then_inc(s_pv, 1)

            def o_of(m):
                return PV[32 * (m % 4):32 * (m % 4) + 32, S * (m // 4):S * (m // 4) + S]

            def hidden(o, i, e, m):
                cols = slice(P * m, P * m + P)
                mm(o[:, :], w01_hi[:, i, e, cols], xw_hi[:, :], start=True, stop=False)
                mm(o[:, :], w01_hi[:, i, e, cols], xw_lo[:, :], start=False, stop=False)
                return mm(o[:, :], w01_lo[:, i, e, cols], xw_hi[:, :], start=False, stop=True)

            def hidden_half(k, q):
                if 0 <= k.i < NK:
                    p, e, m = q // 2, q // 4, (q // 2) % 2
                    kp = k * (NE * NM) + p
                    if q % 2 == 0:
                        if p == 0:
                            pe.wait_ge(s_xw_hi, (k + 1).v)
                            pe.wait_ge(s_xw_lo, (k + 1).v)
                            if k.i == 0:
                                pe.wait_ge(s_part, 4)
                                pe.wait_ge(s_const2, 16 * 4)
                        if kp.i > 0:
                            pe.wait_ge(s_ag, (kp * 1).v)
                        hidden(H0, 0, e, m).then_inc(s_h0, 1)
                    else:
                        if kp.i > 0:
                            pe.wait_ge(s_ug, (kp * 1).v)
                        hidden(H1, 1, e, m).then_inc(s_h1, 1)

            pe.wait_ge(s_const, 16 * 12)
            rows_T(Num(0, 0))
            project(Num(0, 0))
            pe.wait_ge(s_boot, 1)
            for half in range(2):
                stack(Num(0, 0), half)
                for n in range(HU * half, HU * half + HU):
                    rel_logits(Num(0, 0), 0, 0, n)
            stack(Num(0, 0), 2)
            stack(Num(0, 0), 3)
            values(Num(0, 0))

            def body(t):
                lx[0] = [(s_l, t * 32 + 8 if t.i < NK else Num(NU * UH, NU * UH))]
                if 0 <= (t * 2 - 2).i < NB:
                    lx[0].append((s_cnT, t * 2 - 1))
                if t.i == 0:
                    lx[0].append((s_v, Num(1, 1)))
                rt_spread = (t - 2) * NE + 1 if 0 <= (t - 2).i < NK else None
                for s in range(4):
                    u = t * 4 + s
                    half = s % 2
                    for n in range(UH):
                        q = s * UH + n
                        v = u - 1
                        batches = t * 2 + (s + 1) // 2
                        if 0 <= v.i < NU:
                            transposes(v, (s + 1) % 2, n)
                        if q == 31:
                            hidden_half(t - 2, q)
                        if u.i + 1 < NU:
                            rel_logits(u + 1, ((s + 1) // 2) % 2, (s + 1) % 2, n)
                        if u.i < NU:
                            scores(u, (s // 2) % 2, half, n)
                        if 0 <= v.i < NU:
                            band_transposes(v, n, rt_spread)
                            rt_spread = None
                        k = t - 2
                        if q < 31:
                            hidden_half(k, q)
                        if s % 2 == 0:
                            b = t * 2 + s // 2 + 1
                            if b.i < NB:
                                if n == 1:
                                    rows_T(b)
                                if n == 3:
                                    project(b)
                                if n in (5, 6):
                                    stack(b, n - 5)
                        else:
                            b = t * 2 + (s - 1) // 2 + 1
                            if b.i < NB:
                                if n in (0, 1):
                                    stack(b, n + 2)
                                if n == 2:
                                    values(b)
                        if s % 2 == 1:
                            pb = t * 2 + (s - 3) // 2
                            if 0 <= pb.i < NB:
                                if n in (3, 4):
                                    c = n - 3
                                    lx_free()
                                    pe.wait_ge(s_cT, (pb * 2 + 2).v)
                                    for g in range(4):
                                        last = tr(LX[:, P * g:P * g + P], cT[:, g, P * c:P * c + P], ident[:, :])
                                    last.then_inc(s_cx_ps, 1)
                                    lx[0] = [(s_t2, pb * 2 + c + 1)]
                                if n == 6:
                                    lx_free()
                                    pe.wait_ge(s_cn, (pb * 2 + 2).v)
                                    for c in range(NC):
                                        last = tr(LX[:, P * c:P * c + P], cn[:, c, :], ident[:, :])
                                    last.then_inc(s_cnT_ps, 1)
                                    lx[0] = [(s_cnT, pb + 1)]
                            pb = t * 2 + (s - 1) // 2 - 2
                            if n == 5 and 0 <= pb.i < NB:
                                lx_free()
                                pe.wait_ge(s_wl, (pb + 1).v)
                                for c in range(NC):
                                    last = tr(LX[0:2 * NE, P * c:P * c + P], wr[:, c, :].bitcast(F32), ident[:, :])
                                last.then_inc(s_ws_ps, 1)
                                lx[0] = [(s_ws, pb + 1)]
                        else:
                            pb = t * 2 + s // 2 - 2
                            if 0 <= pb.i < NB:
                                if n == 0:
                                    lx_free()
                                    if pb.i == 0:
                                        pe.wait_ge(s_const2, 16 * 4)
                                    pe.wait_ge(s_cnT, (pb + 1).v)
                                    for c in range(NC):
                                        last = mm(LX[:, P * c:P * c + P], cnT[:, P * c:P * c + P], wout_sb[:, :],
                                                  start=True, stop=True)
                                    last.then_inc(s_op_ps, 1)
                                    lx[0] = [(s_x1, pb + 1)]
                                if n == 2:
                                    lx_free()
                                    pe.wait_ge(s_xn2, (pb * 2 + 2).v)
                                    for c in range(NC):
                                        last = tr(LX[:, P * c:P * c + P], xn2[:, c, :], ident[:, :])
                                    last.then_inc(s_xs_ps, 1)
                                    lx[0] = [(s_xs, pb + 1)]
                                if n == 4:
                                    lx_free()
                                    pe.wait_ge(s_xs, (pb + 1).v)
                                    o = BT // 2 * ((s // 2) % 2)
                                    for c in range(NC):
                                        last = mm(LX[:, NE * c:NE * c + NE], xs[:, o + P * c:o + P * c + P],
                                                  gate_sb[:, :], start=True, stop=True)
                                    last.then_inc(s_g_ps, 1)
                                    lx[0] = [(s_lg, pb + 1)]
                        kf = t - 3
                        if s == 1 and n == 7 and 0 <= kf.i < NK:
                            lx_free()
                            pe.wait_ge(s_oT, (kf + 1).v)
                            for i in range(4):
                                last = tr(LX[:, P * i:P * i + P], oT[:, P * i:P * i + P], ident[:, :])
                            last.then_inc(s_f_ps, 1)
                            lx[0] = [(s_fin, kf + 1)]
                        ko, po = (k, q // 2 - 1) if q > 0 else (k - 1, NE * NM - 1)
                        if q % 2 == 0 and 0 <= ko.i < NK:
                            pe.wait_ge(s_ug, (ko * (NE * NM) + (po + 1)).v)
                            if po == 0 and ko.i > 0:
                                pe.wait_ge(s_oT, (ko * 1).v)
                            mm(OB[:, :], wo_sb[:, po // NM, po % NM, :], ug,
                               start=(po == 0), stop=(po == NE * NM - 1)).then_inc(s_wo, 1)
                        for kk, ee in ([(k, q // 4 + 1)] if q % 4 == 1 and q < 28 else [(k + 1, 0)] if q == 31 else []):
                            if 0 <= kk.i < NK:
                                x_e = kk * NE + ee
                                if u.i - 1 < NU and u.i >= 1:
                                    pe.wait_ge(s_rt, ((u - 1) * UH + n + 1).v)
                                if x_e.i > 0:
                                    pe.wait_ge(s_we, (x_e * 1).v)
                                if ee == 0:
                                    pe.wait_ge(s_ww, (kk + 1).v)
                                mm(RT[:, :], pick[:, ee, :], ww[:, :], start=True, stop=True).then_inc(s_wb_ps, 1)
                                rt_spread = x_e + 1
                        if 0 <= v.i < NU and n % 2 == 1:
                            context(v, batches, ((s - 1) // 2) % 2, (s + 1) % 2, n - 1)

            iterations(pe, body)

        @block.scalar
        def _(act):
            f = nc.scalar.activation

            def take_xnT(b):
                act.wait_ge(s_xnT_ps, (b + 1).v)
                if b.i >= 1:
                    act.wait_ge(s_v_ps, (b * 1).v)
                if b.i >= 3:
                    act.wait_ge(s_op_ps, (b - 2).v)
                f(xnT[:, :], LX[:, 0:S], ACT.Copy).then_inc(s_xnT, 1)

            def hi_parts(b):
                act.wait_ge(s_qk32, (b * 2 + 2).v)
                if b.i >= 1:
                    act.wait_ge(s_stk_ps, (b * 4).v)
                f(qk_hi[:, :, :], qk32[:, :, :], ACT.Copy).then_inc(s_hi, 1)

            def take_stack(b, par, g):
                act.wait_ge(s_stk_ps, (b * 4 + g + 1).v)
                f(qk[:, par, g, :, :], LX[:, :].rearrange("p (w s) -> p w s", w=2), ACT.Copy).then_inc(s_stk, 1)

            take_xnT(Num(0, 0))
            hi_parts(Num(0, 0))
            act.wait_ge(s_boot, 1)
            for g in range(4):
                take_stack(Num(0, 0), 0, g)

            def body(t):
                for s in range(4):
                    u = t * 4 + s
                    for n in range(UH):
                        q = s * UH + n
                        k = t - 2
                        if q % 2 == 1 and 0 <= k.i < NK:
                            kp = k * 16 + q // 2
                            act.wait_ge(s_h0, (kp + 1).v)
                            if kp.i > 0:
                                act.wait_ge(s_ug, (kp * 1).v)
                            f(th, H0[:, :], ACT.Tanh, scale=0.5).then_inc(s_th, 1)
                        if s % 2 == 0 and n == 4 and (t * 2 + s // 2 + 1).i < NB:
                            hi_parts(t * 2 + s // 2 + 1)
                        v = u - 1
                        if 0 <= v.i < NU:
                            hp = n % 2
                            act.wait_ge(s_pt_ps, (v * UH + n + 1).v)
                            if v.i > 0 or n > 1:
                                act.wait_ge(s_pv, (v * UH + n - 1).v)
                            f(pT[:, hp, :, :], PT[:, :].rearrange("p (c s) -> p c s", c=NC), ACT.Copy).then_inc(s_pt, 1)
                            act.wait_ge(s_rt_ps, (v * UH + n + 1).v)
                            f(rT[:, hp, :], RT[:, 0:S], ACT.Copy).then_inc(s_rt, 1)
                        kn = t - 1
                        if q == 31 and 0 <= kn.i < NK:
                            act.wait_ge(s_xs, (kn * 2 + 2).v)
                            if kn.i >= 1:
                                act.wait_ge(s_h1, (kn * 16).v)
                            f(xw_hi[:, :], xs[:, :], ACT.Copy).then_inc(s_xw_hi, 1)
                        if q == 1 and 0 <= t.i - 3 < NK:
                            act.wait_ge(s_wo, ((t - 3) * 16 + 16).v)
                            if t.i > 3:
                                act.wait_ge(s_f_ps, (t - 3).v)
                            f(oT, OB[:, :], ACT.Copy).then_inc(s_oT, 1)
                        if u.i < NU:
                            if n == 0 and u.i >= 2:
                                act.wait_ge(s_pt_ps, ((u - 1) * UH).v)
                                for half in range(2):
                                    act.wait_ge(s_pw[half], ((u - 1) * 32).v)
                            for c in range(NC):
                                act.wait_ge(s_ttr, (u * 16 + 2 * n + c + 1).v)
                                f(prob[:, s % 2, c, n, :], sneg[:, n % 2, c, :], ACT.Exp,
                                  bias=nmax[:, n % 2, c:c + 1], scale=-1.0).then_inc(s_exp, 1)
                        for kk, ee in ([(k, q // 4 + 1)] if q % 4 == 1 and q < 28 else [(k + 1, 0)] if q == 31 else []):
                            if 0 <= kk.i < NK:
                                x_e = kk * NE + ee
                                act.wait_ge(s_wb_ps, (x_e + 1).v)
                                if x_e.i >= 2:
                                    act.wait_ge(s_agw, ((x_e - 1) * NM).v)
                                f(we[:, ee % 2, :], RT[:, :], ACT.Copy).then_inc(s_we, 1)
                        if 0 <= v.i < NU and n == UH - 1:
                            act.wait_ge(s_pv, (v * UH + UH).v)
                            if s % 2 == 1 and v.i >= 2:
                                act.wait_ge(s_cx_ps, ((t * 2 + (s - 3) // 2) * 2 + 2).v)
                            g = 2 * ((s + 1) % 2)
                            f(cT[:, g:g + 2, :], PV[:, :].rearrange("p (g s) -> p g s", g=2), ACT.Copy).then_inc(s_cT, 1)
                        if s % 2 == 0:
                            b = t * 2 + s // 2 + 1
                            par = (s // 2 + 1) % 2
                            if b.i < NB:
                                if n == 1:
                                    take_xnT(b)
                                if n == 5:
                                    take_stack(b, par, 0)
                            pb = t * 2 + s // 2 - 2
                            if 0 <= pb.i < NB:
                                o = BT // 2 * ((s // 2) % 2)
                                if n == 2:
                                    act.wait_ge(s_xs_ps, (pb + 1).v)
                                    if pb.i >= 2:
                                        act.wait_ge(s_xw_hi, ((t - 2) + 1).v)
                                        act.wait_ge(s_xw_lo, ((t - 2) + 1).v)
                                    f(xs[:, o:o + S], LX[:, 0:S], ACT.Copy).then_inc(s_xs, 1)
                                if n == 6:
                                    act.wait_ge(s_gd, (pb + 1).v)
                                    f(ge[:, :], gd[:, :], ACT.Exp).then_inc(s_ge, 1)
                        else:
                            b = t * 2 + (s - 1) // 2 + 1
                            par = ((s - 1) // 2 + 1) % 2
                            if b.i < NB and n == 0:
                                take_stack(b, par, 2)
                            pb = t * 2 + (s - 3) // 2
                            if 0 <= pb.i < NB and n == 6:
                                act.wait_ge(s_cnT_ps, (pb + 1).v)
                                act.wait_ge(s_v_ps, (pb + 3).v if pb.i + 2 < NB else NB)
                                f(cnT[:, :], LX[:, 0:S], ACT.Copy).then_inc(s_cnT, 1)
                            pb = t * 2 + (s - 1) // 2 - 2
                            if 0 <= pb.i < NB and n == 5:
                                o = BT // 2 * (((s - 1) // 2) % 2)
                                act.wait_ge(s_ws_ps, (pb + 1).v)
                                if pb.i >= 2:
                                    act.wait_ge(s_ww, ((t - 2) + 1).v)
                                f(ws[:, o:o + S], LX[0:2 * NE, 0:S], ACT.Copy).then_inc(s_ws, 1)

            iterations(act, body)

        @block.vector
        def _(dve):
            counts = [dve.alloc_register(f"dve_count{i}") for i in range(3)]
            V = nc.vector

            def sums(b, loads, par):
                dve.wait_ge(s_x[par], (loads * 16).v)
                if b.i >= 1:
                    dve.wait_ge(s_mv, (b * 2).v)
                for c in range(NC):
                    V.bn_stats(stat[:, c, :], xt[:, par, c, :]).then_inc(s_st, 1)

            def aggregate(b):
                ready0 = counted(dve, counts[0], b * 2 + 2)
                if b.i >= 1:
                    ready1 = counted(dve, counts[1], b * 2)
                dve.wait_ge(s_const, 16 * 12)
                dve.wait_ge(s_st, ready0)
                if b.i >= 1:
                    dve.wait_ge(s_xn, ready1)
                for c in range(NC):
                    V.bn_aggr(mv[:, c, :], stat[:, c, :]).then_inc(s_mv, 1)

            def normalise(b, par):
                dve.wait_ge(s_rs, (b + 1).v)
                if b.i >= 1:
                    dve.wait_ge(s_xnT_ps, (b * 1).v)
                for c in range(NC):
                    V.tensor_scalar(xn[:, c, :], xt[:, par, c, :], mv[:, c, 0:1], rstd[:, c:c + 1],
                                    ALU.subtract, ALU.mult).then_inc(s_xn, 1)

            def take_qk(b):
                dve.wait_ge(s_qk_ps, (b + 1).v)
                if b.i >= 1:
                    dve.wait_ge(s_lo, (b * 1).v)
                    dve.wait_ge(s_hi, (b * 1).v)
                V.tensor_scalar(qk32[:, 0, :], LX[:, 0:S], bqk_sb[:, 0:1], float(HD) ** -0.5,
                                ALU.add, ALU.mult).then_inc(s_qk32, 1)
                V.tensor_scalar(qk32[:, 1, :], LX[:, S:2 * S], bqk_sb[:, 1:2], None, ALU.add).then_inc(s_qk32, 1)

            def lo_parts(b):
                dve.wait_ge(s_hi, (b + 1).v)
                if b.i >= 1:
                    dve.wait_ge(s_stk_ps, (b * 4).v)
                V.tensor_tensor(qk_lo[:, :, :], qk32[:, :, :], qk_hi[:, :, :].bitcast(F32),
                                ALU.subtract).then_inc(s_lo, 1)

            def take_stack(b, par, g):
                dve.wait_ge(s_stk_ps, (b * 4 + g + 1).v)
                V.tensor_copy(qk[:, par, g, :, :], LX[:, :].rearrange("p (w s) -> p w s", w=2)).then_inc(s_stk, 1)

            def take_values(b, par):
                dve.wait_ge(s_v_ps, (b + 1).v)
                if b.i >= 2:
                    dve.wait_ge(s_pv, ((b - 1) * 16).v)
                V.tensor_tensor(val[:, par, :, :, 0:HD],
                                LX[:, 0:2 * D].rearrange("p (c h d) -> p c h d", c=NC, d=HD),
                                bv_sb[:, :].rearrange("p (h d) -> p h d", d=HD).unsqueeze(1).to_broadcast([P, NC, H, HD]),
                                ALU.add).then_inc(s_v, 1)

            def take_l(u, n):
                dve.wait_ge(s_l_ps, (u * UH + n + 1).v)
                if n % 4 == 0 and u.i >= 1:
                    dve.wait_ge(s_lw[n // 4], (u * 32).v)
                V.tensor_copy(lrow[:, n // 4, :, n % 4, :],
                              LX[:, 0:2 * WIN].rearrange("p (c w) -> p c w", c=NC)).then_inc(s_l, 1)

            b0 = Num(0, 0)
            V.memset(val[:, :, :, :, :], 0.0).then_inc(s_const_dve, 1)
            V.memset(ev[:, :, :], 0.0).then_inc(s_const_dve, 1)
            V.memset(bias[:, 0, :, WIN:S], 0.0)
            V.memset(bias[:, 1, :, 0:R], 0.0).then_inc(s_const_dve, 1)
            dve.wait_ge(s_const_dve, 3)
            V.memset(val[:, :, :, :, HD:HD + 1], 1.0)
            sums(b0, b0 + 1, 0)
            aggregate(b0)
            normalise(b0, 0)
            dve.wait_ge(s_const, 16 * 12)
            V.tensor_copy(sel[:, :, :].rearrange("p g m -> p (g m)"), sel_f)
            V.tensor_copy(pick[:, :, :].rearrange("p e m -> p (e m)"), pick_f)
            for c in range(NC):
                V.tensor_scalar(ek_w[:, c, :], ek_w[:, c, :], ek_r[:, c:c + 1], None,
                                ALU.subtract).then_inc(s_const_dve, 1)
            dve.wait_ge(s_const_dve, 5)
            V.tensor_copy(ek_hi[:, :, :], ek_w[:, :, :]).then_inc(s_const_dve, 1)
            take_qk(b0)
            dve.wait_ge(s_const_dve, 6)
            V.tensor_tensor(ek_w[:, :, :], ek_w[:, :, :], ek_hi[:, :, :].bitcast(F32),
                            ALU.subtract).then_inc(s_const_dve, 1)
            V.tensor_scalar(ek_hi[:, :, :], ek_hi[:, :, :].bitcast(F32), mask[:, 0:1], None,
                            ALU.mult).then_inc(s_const_dve, 1)
            dve.wait_ge(s_const_dve, 8)
            V.scalar_tensor_tensor(ek[:, :, :], ek_w[:, :, :], mask[:, 1:2], ek_hi[:, :, :].bitcast(F32),
                                   ALU.mult, ALU.add)
            for c in range(NC):
                V.tensor_tensor(ev[:, c, 0:HD], ev_r[:, :], edge[:, 1 - c, 0:HD], ALU.subtract)
                V.tensor_tensor(ev_tail[:, c, :], edge[:, c, :], edge[:, 1 - c, :],
                                ALU.subtract).then_inc(s_const_dve, 1)
            lo_parts(b0)
            V.memset(cn[:, :, :], 0.0).then_inc(s_boot, 1)
            sums(b0 + 1, b0 + 1, 1)
            aggregate(b0 + 1)
            for n in range(UH):
                take_l(b0, n)
            take_values(b0, 0)

            def head_logits(u, n):
                ready0 = counted(dve, counts[0], u * UH + n + 1)
                if n % 4 == 0:
                    ready1 = counted(dve, counts[1], u * 32 + 32)
                if u.i > 0 or n > 1:
                    ready2 = counted(dve, counts[2], u * 16 + 2 * n - 2)
                dve.wait_ge(s_const, 16 * 12)
                dve.wait_ge(s_s, ready0)
                if n % 4 == 0:
                    dve.wait_ge(s_br[n // 4], ready1)
                if u.i > 0 or n > 1:
                    dve.wait_ge(s_exp, ready2)
                for c in range(NC):
                    V.tensor_tensor_reduce(out=sneg[:, n % 2, c, :], in0=SB_[:, S * c:S * c + S],
                                           in1=bias[:, c, n, :], scale=-1.0, scalar=BIG,
                                           op0=ALU.add, op1=ALU.min,
                                           accum_out=nmax[:, n % 2, c:c + 1]).then_inc(s_ttr, 1)

            def tails(u, slot, n, prev, at):
                hf = n // 4
                dve.wait_ge(s_pr[hf], (u * 32 + 32).v)
                bp = ((slot - 1) // 2) % 2
                h0 = UH * ((slot + 1) % 2) + HU * hf
                if prev is not None and prev.i > 0:
                    dve.wait_ge(s_t1, prev.v)
                V.tensor_reduce(tail[:, bp, at // P, h0:h0 + HU],
                                prel[:, at // P, HU * hf:HU * hf + HU, at:at + R],
                                AX.X, ALU.add).then_inc(s_tail, 1)

            def x1_stats(b):
                dve.wait_ge(s_x1, (b + 1).v)
                for c in range(NC):
                    V.bn_stats(stat2[:, c, :], x1[:, c, :]).then_inc(s_st2, 1)

            def x1_aggr(b):
                ready = counted(dve, counts[0], b * 2 + 2)
                dve.wait_ge(s_const, 16 * 12)
                dve.wait_ge(s_st2, ready)
                for c in range(NC):
                    V.bn_aggr(mv2[:, c, :], stat2[:, c, :]).then_inc(s_mv2, 1)

            def x1_normalise(b):
                dve.wait_ge(s_rs2, (b + 1).v)
                if b.i >= 1:
                    dve.wait_ge(s_xs_ps, (b * 1).v)
                for c in range(NC):
                    V.tensor_scalar(xn2[:, c, :], x1[:, c, :], mv2[:, c, 0:1], rstd2[:, c:c + 1],
                                    ALU.subtract, ALU.mult).then_inc(s_xn2, 1)

            def gate_top(b):
                ready = counted(dve, counts[0], b + 1)
                dve.wait_ge(s_const, 16 * 12)
                dve.wait_ge(s_lg, ready)
                for c in range(NC):
                    V.max(top[:, c, :], lg[:, c, :]).then_inc(s_top, 1)

            def gate_place(b):
                ready = counted(dve, counts[0], b * 2 + 2)
                dve.wait_ge(s_const, 16 * 12)
                dve.wait_ge(s_top, ready)
                for c in range(NC):
                    V.max_index(topi[:, c, :], top[:, c, :], lg[:, c, :]).then_inc(s_topi, 1)
                V.tensor_tensor(gd[:, :], top[:, :, 1], top[:, :, 0], ALU.subtract).then_inc(s_gd, 1)

            def gate_place_float(b):
                dve.wait_ge(s_topi, (b * 2 + 2).v)
                V.tensor_copy(topf[:, :, :], topi[:, :, :]).then_inc(s_topf, 1)

            def gate_sum(b):
                dve.wait_ge(s_ge, (b + 1).v)
                V.tensor_scalar(gs[:, :], ge[:, :], 2.0, 2.0, ALU.mult, ALU.add).then_inc(s_gs, 1)

            def gate_first(b):
                dve.wait_ge(s_gs, (b + 1).v)
                V.reciprocal(gp[:, 0, :], gs[:, :]).then_inc(s_gp1, 1)

            def gate_second(b):
                dve.wait_ge(s_gp1, (b + 1).v)
                V.tensor_tensor(gp[:, 1, :], ge[:, :], gp[:, 0, :], ALU.mult).then_inc(s_gp2, 1)

            def gate_one_hot(b):
                dve.wait_ge(s_topf, (b + 1).v)
                dve.wait_ge(s_gp2, (b + 1).v)
                for c in range(NC):
                    for i, w_ in ((0, wa), (1, wb)):
                        V.tensor_scalar(w_[:, c, :], iota[:, :], topf[:, c, i:i + 1],
                                        gp[:, i, c:c + 1], ALU.is_equal, ALU.mult).then_inc(s_oh, 1)

            def gate_weights(b):
                dve.wait_ge(s_oh, (b * 4 + 4).v)
                V.tensor_tensor(wf[:, :, :], wa[:, :, :], wb[:, :, :], ALU.add).then_inc(s_wf, 1)

            def gate_hi(b):
                dve.wait_ge(s_wf, (b + 1).v)
                if b.i >= 1:
                    dve.wait_ge(s_ws_ps, (b * 1).v)
                V.tensor_copy(wr[:, :, 0:NE], wf[:, :, :]).then_inc(s_wh, 1)

            def gate_lo(b):
                dve.wait_ge(s_wh, (b + 1).v)
                V.tensor_tensor(wr[:, :, NE:2 * NE], wf[:, :, :], wr[:, :, 0:NE].bitcast(F32),
                                ALU.subtract).then_inc(s_wl, 1)

            EVEN = {(1, 0): x1_stats, (1, 1): x1_aggr, (2, 0): x1_normalise, (5, 0): gate_top, (5, 1): gate_place,
                    (6, 0): gate_place_float, (7, 0): gate_sum, (7, 1): gate_first}
            ODD = {(0, 0): gate_second, (0, 1): gate_one_hot, (1, 0): gate_weights, (1, 1): gate_hi, (2, 0): gate_lo}

            def context_sum(b, c):
                i = b * 2 + c
                rows = LX[:, :].rearrange("p (h v) -> p h v", v=VS)
                dve.wait_ge(s_cx_ps, (i + 1).v)
                dve.wait_ge(s_t1, (i + 1).v)
                if i.i > 0:
                    dve.wait_ge(s_t3, (i * 1).v)
                V.reciprocal(rz[:, :], rows[:, :, HD]).then_inc(s_rz, 1)
                if b.i >= 1:
                    dve.wait_ge(s_cnT_ps, (b * 1).v)
                V.tensor_tensor(t2[:, c, :].rearrange("p (h d) -> p h d", d=HD), rows[:, :, 0:HD],
                                t1[:, c, :].rearrange("p (h d) -> p h d", d=HD), ALU.add).then_inc(s_t2, 1)

            def context_scale(b, c):
                i = b * 2 + c
                dve.wait_ge(s_rz, (i + 1).v)
                dve.wait_ge(s_t2, (i + 1).v)
                V.tensor_tensor(t3[:, c, :].rearrange("p (h d) -> p h d", d=HD),
                                t2[:, c, :].rearrange("p (h d) -> p h d", d=HD),
                                rz[:, :].unsqueeze(2).to_broadcast([P, H, HD]), ALU.mult).then_inc(s_t3, 1)

            def body(t):
                for s in range(4):
                    u = t * 4 + s
                    v = u - 1
                    even = s % 2 == 0
                    b = t * 2 + s // 2 + 1
                    par = (s // 2 + 1) % 2
                    pb = t * 2 + s // 2 - 2
                    cb = t * 2 + (s - 3) // 2
                    for n in range(UH):
                        q = s * UH + n
                        k = t - 2

                        def small(half_step):
                            stage = (EVEN if even else ODD).get((n, half_step))
                            if stage is not None and 0 <= pb.i < NB:
                                stage(pb)
                            if not even and 0 <= cb.i < NB and half_step == 0 and n in (4, 5):
                                context_scale(cb, n - 4)
                            if even and b.i < NB and (n, half_step) == (4, 1):
                                lo_parts(b)
                            if even and b.i < NB and (n, half_step) == (0, 1):
                                normalise(b, par)
                            nb = b + 1
                            if not even and nb.i < NB and (n, half_step) == (5, 1):
                                sums(nb, t + 2, (par + 1) % 2)
                            if not even and nb.i < NB and (n, half_step) == (6, 1):
                                aggregate(nb)
                            if s == 3 and (n, half_step) == (6, 0) and 0 <= (t - 1).i < NK:
                                dve.wait_ge(s_ws, (t * 2).v)
                                if (t - 1).i >= 1:
                                    dve.wait_ge(s_wb_ps, ((t - 1) * NE).v)
                                V.tensor_copy(ww[:, :], ws[:, :]).then_inc(s_ww, 1)
                            if 0 <= v.i < NU and n in (1, 5):
                                prev = (t * 2 + (s - 1) // 2) * 2 - 2 if v.i >= 4 and n == 1 and not even else None
                                tails(v, s, n, prev, P * half_step)

                        ko, po = (k, q // 2 - 1) if q > 0 else (k - 1, NE * NM - 1)
                        if q % 2 == 0 and 0 <= ko.i < NK:
                            kp = ko * 16 + po
                            dve.wait_ge(s_agw, (kp + 1).v)
                            dve.wait_ge(s_h1, (kp + 1).v)
                            if kp.i >= 1:
                                dve.wait_ge(s_wo, (kp * 1).v)
                            V.tensor_tensor(ug, th, H1[:, :], ALU.mult).then_inc(s_ug, 1)
                        l_first = n == (3 if even else 1)
                        if u.i + 1 < NU and l_first:
                            take_l(u + 1, n)
                        if q % 2 == 1 and 0 <= k.i < NK:
                            kp = k * 16 + q // 2
                            dve.wait_ge(s_th, (kp + 1).v)
                            V.scalar_tensor_tensor(th, th, 1.0, H0[:, :], ALU.add,
                                                   ALU.mult).then_inc(s_ag, 1)
                            if t.i >= NK:
                                dve.wait_ge(s_ag, (kp + 1).v)
                                dve.wait_ge(s_we, (k * NE + (q // 4 + 1)).v)
                                V.tensor_tensor(th, th, we[:, (q // 4) % 2, :], ALU.mult).then_inc(s_agw, 1)
                        if u.i + 1 < NU and not l_first:
                            take_l(u + 1, n)
                        small(0)
                        if u.i < NU:
                            head_logits(u, n)
                        small(1)
                        if even and b.i < NB:
                            if n == 3:
                                take_qk(b)
                            if n == 6:
                                take_stack(b, par, 1)
                        if even and 0 <= pb.i < NB:
                            if n == 0:
                                dve.wait_ge(s_op_ps, (pb + 1).v)
                                dve.wait_ge(s_xb, (pb + 1).v)
                                if pb.i >= 1:
                                    dve.wait_ge(s_x1w, (pb * 16).v)
                                    dve.wait_ge(s_xn2, (pb * 2).v)
                                V.tensor_tensor(x1[:, :, :], LX[:, 0:2 * D].rearrange("p (c d) -> p c d", c=NC),
                                                xb[:, :, :], ALU.add).then_inc(s_x1, 1)
                            if n == 4:
                                dve.wait_ge(s_g_ps, (pb + 1).v)
                                V.tensor_copy(lg[:, :, :], LX[:, 0:2 * NE].rearrange("p (c e) -> p c e", c=NC)) \
                                    .then_inc(s_lg, 1)
                        if not even and b.i < NB:
                            if n == 1:
                                take_stack(b, par, 3)
                            if n == 2:
                                take_values(b, par)
                        if not even and 0 <= cb.i < NB and n in (3, 4):
                            context_sum(cb, n - 3)
                        kf = t - 3
                        if s == 1 and n == 7 and 0 <= kf.i < NK:
                            dve.wait_ge(s_f_ps, (kf + 1).v)
                            dve.wait_ge(s_xo, (kf * 16 + 16).v)
                            V.tensor_tensor(xo[:, :, :], LX[:, :].rearrange("p (j d) -> p j d", d=D), xo[:, :, :],
                                            ALU.add).then_inc(s_fin, 1)
                        kn = t - 1
                        if q == 31 and 0 <= kn.i < NK:
                            dve.wait_ge(s_xw_hi, (kn + 1).v)
                            V.tensor_tensor(xw_lo[:, :], xs[:, :], xw_hi[:, :].bitcast(F32),
                                            ALU.subtract).then_inc(s_xw_lo, 1)

            iterations(dve, body)


def kernel(L0_attn_x, L0_attn_W_qkv, L0_attn_b_qkv, L0_attn_W_out, L0_attn_b_out, L0_attn_rel_emb_k,
           L0_attn_rel_emb_v, L0_ffn_gate_kernel, L0_ffn_w0_kernel, L0_ffn_w1_kernel, L0_ffn_wo_kernel):
    import concourse.bacc as bacc
    from concourse.bass_utils import run_bass_kernel_spmd

    def c_(a):
        return np.ascontiguousarray(a)

    b_qkv = np.asarray(L0_attn_b_qkv)
    rk, rv = np.asarray(L0_attn_rel_emb_k), np.asarray(L0_attn_rel_emb_v)
    w = np.arange(WIN)
    offs = (np.clip(w - R + 1, 0, 2 * R), np.minimum(w + 1, 2 * R))
    refs = (2 * R, 0)
    d_of = np.arange(P) % HD
    ek_win = c_(np.stack([rk[o][:, d_of].T for o in offs], axis=1))
    ek_ref = c_(np.stack([rk[r][d_of] for r in refs], axis=1))
    ev_edge = c_(np.stack([np.broadcast_to(np.tile(rv[r], H), (P, D)) for r in (0, 2 * R)], axis=1))
    sel = np.zeros((P, 16, P), np.float32)
    for g in range(4):
        for kind, parts in enumerate(((0, 1), (2, 3), (0, 2), (1, 3))):
            for j in range(4):
                for s in parts:
                    for d in range(HD):
                        sel[HD * (4 * g + j) + d, 4 * g + kind, 32 * j + HD * s + d] = 1.0
    pick = np.zeros((2 * NE, NE, P), np.float32)
    for e in range(NE):
        pick[e, e], pick[NE + e, e] = 1.0, 1.0
    part = (np.arange(P) % 32) // HD
    mask = c_(np.stack([part % 2 == 0, part % 2 == 1], axis=1).astype(np.float32))
    arrays = {
        "x": c_(np.asarray(L0_attn_x).reshape(NB * S, D)), "w_qkv": c_(L0_attn_W_qkv), "w_out": c_(L0_attn_W_out),
        "gate": c_(L0_ffn_gate_kernel), "w0": c_(L0_ffn_w0_kernel), "w1": c_(L0_ffn_w1_kernel),
        "wo": c_(L0_ffn_wo_kernel), "bqk": c_(b_qkv[:2 * D].reshape(2, D).T),
        "bv": c_(np.broadcast_to(b_qkv[2 * D:], (P, D))), "bout": c_(np.broadcast_to(np.asarray(L0_attn_b_out), (P, D))),
        "ek_win": ek_win, "ek_ref": ek_ref, "ev_rows": c_(rv[1:]), "ev_edge": ev_edge,
        "ident_in": np.eye(P, dtype=np.float32), "sel_in": sel, "pick_in": pick,
        "iota_in": c_(np.broadcast_to(np.arange(NE, dtype=np.float32), (P, NE))), "mask_in": mask,
    }
    nc = bacc.Bacc("TRN2", target_bir_lowering=False, num_devices=1)
    aps = [nc.dram_tensor(n, a.shape, mybir.dt.from_np(a.dtype), kind="ExternalInput").ap() for n, a in arrays.items()]
    out = nc.dram_tensor("out", (NB * S, D), F32, kind="ExternalOutput").ap()
    layer_program(nc, *aps, out)
    r = run_bass_kernel_spmd(nc, [arrays], core_ids=[0])
    return r.results[0]["out"].reshape(NB, S, D)
```
